# Optimizing a Trainium2 kernel written in Bass

```python
import numpy as np
import jax
import jax.numpy as jnp

def _softmax(x, axis=-1):
    return jax.nn.softmax(x, axis=axis)

def _gelu(x):
    return jax.nn.gelu(x, approximate=True)

def _silu(x):
    return jax.nn.silu(x)

def _sigmoid(x):
    return jax.nn.sigmoid(x)

def _layernorm(x, axis=-1, eps=1e-05):
    m = jnp.mean(x, axis=axis, keepdims=True)
    v = jnp.var(x, axis=axis, keepdims=True)
    return (x - m) / jnp.sqrt(v + eps)

def _scatter_add(tgt, idx, src, axis=0):
    return tgt.at[idx].add(src)

def _segment_sum(src, seg, n):
    return jax.ops.segment_sum(src, seg, n)
kernel_name = 'mk_metaformer_d1_conv_nchw512_r2_c18b30'

def setup_inputs(seed: int=0):
    np.random.seed(seed)
    _w = jnp.asarray

    def _rec_inputs():
        import jax
        import jax.numpy as jnp
        _gk = jax.random.key(seed)
        x = -0.0003929 + 0.9999 * jax.random.normal(jax.random.fold_in(_gk, 1), (8, 256, 32, 32), jnp.float32)
        return x
    x = _rec_inputs()

    def _L0_conv_setup():
        import jax, jax.numpy as jnp
        import numpy as np
        DIM = 8
        EPS_ATT = 1e-15
        BN_EPS = 1e-05

        def conv2d(x, w, groups=1, padding=0):
            return jax.lax.conv_general_dilated(x, w, window_strides=(1, 1), padding=[(padding, padding), (padding, padding)], dimension_numbers=('NCHW', 'OIHW', 'NCHW'), feature_group_count=groups)
        key = jax.random.key(seed)
        ks = jax.random.split(key, 8)
        B, C, H, W = (8, 256, 32, 32)
        TD = 256
        s = lambda k, shape, fan: jax.random.normal(k, shape, jnp.float32) * (1.0 / np.sqrt(fan))
        return {'x': jax.random.normal(ks[0], (B, C, H, W), jnp.float32), 'qkv_w': s(ks[1], (3 * TD, C, 1, 1), C), 'agg_dw_w': s(ks[2], (3 * TD, 1, 5, 5), 25), 'agg_pw_w': s(ks[3], (3 * TD, 3 * TD // (3 * 32), 1, 1), 8), 'proj_w': s(ks[4], (C, 2 * TD, 1, 1), 2 * TD), 'bn_gamma': jnp.ones((C,), jnp.float32), 'bn_beta': jnp.zeros((C,), jnp.float32), 'bn_mean': jax.random.normal(ks[5], (C,), jnp.float32) * 0.1, 'bn_var': jax.random.uniform(ks[6], (C,), jnp.float32, 0.5, 1.5)}
    _L0_conv_all = _L0_conv_setup()
    _L0_conv_in = {k: v for k, v in _L0_conv_all.items() if k in ('qkv_w', 'agg_dw_w', 'agg_pw_w', 'proj_w', 'bn_gamma', 'bn_beta', 'bn_mean', 'bn_var')}
    del _L0_conv_all

    def _L0_ffn_setup():
        import jax, jax.numpy as jnp
        import numpy as np
        N_CONST = 6
        PARTITIONS_OF_6 = [(6,), (5, 1), (4, 2), (4, 1, 1), (3, 3), (3, 2, 1), (3, 1, 1, 1), (2, 2, 2), (2, 2, 1, 1), (2, 1, 1, 1, 1), (1, 1, 1, 1, 1, 1)]
        N_EXPERTS = 6
        TOP_K = 2

        def _partition_weights():
            w = np.zeros((len(PARTITIONS_OF_6), N_EXPERTS), dtype=np.float32)
            for i, partition in enumerate(PARTITIONS_OF_6):
                for j, part in enumerate(partition):
                    if j < N_EXPERTS:
                        w[i, j] = part / N_CONST
            return jnp.asarray(w)
        key = jax.random.key(seed)
        ks = jax.random.split(key, 6)
        B, S, D, F, E, P = (32, 1024, 256, 341, 6, 11)
        scale_in = 1.0 / np.sqrt(D)
        scale_hid = 1.0 / np.sqrt(F)
        return {'x': jax.random.normal(ks[0], (B, S, D), dtype=jnp.float32), 'router_w': jax.random.normal(ks[1], (P, D), dtype=jnp.float32) * scale_in, 'W1': jax.random.normal(ks[2], (E, D, F), dtype=jnp.float32) * scale_in, 'b1': jax.random.normal(ks[3], (E, F), dtype=jnp.float32) * 0.01, 'W2': jax.random.normal(ks[4], (E, F, D), dtype=jnp.float32) * scale_hid, 'b2': jax.random.normal(ks[5], (E, D), dtype=jnp.float32) * 0.01}
    _L0_ffn_all = _L0_ffn_setup()
    _L0_ffn_in = {k: v for k, v in _L0_ffn_all.items() if k in ('router_w', 'W1', 'b1', 'W2', 'b2')}
    del _L0_ffn_all
    return {'x': x, 'L0_conv_qkv_w': _L0_conv_in['qkv_w'], 'L0_conv_agg_dw_w': _L0_conv_in['agg_dw_w'], 'L0_conv_agg_pw_w': _L0_conv_in['agg_pw_w'], 'L0_conv_proj_w': _L0_conv_in['proj_w'], 'L0_conv_bn_gamma': _L0_conv_in['bn_gamma'], 'L0_conv_bn_beta': _L0_conv_in['bn_beta'], 'L0_conv_bn_mean': _L0_conv_in['bn_mean'], 'L0_conv_bn_var': _L0_conv_in['bn_var'], 'L0_ffn_router_w': _L0_ffn_in['router_w'], 'L0_ffn_W1': _L0_ffn_in['W1'], 'L0_ffn_b1': _L0_ffn_in['b1'], 'L0_ffn_W2': _L0_ffn_in['W2'], 'L0_ffn_b2': _L0_ffn_in['b2']}

def reference(x, L0_conv_qkv_w, L0_conv_agg_dw_w, L0_conv_agg_pw_w, L0_conv_proj_w, L0_conv_bn_gamma, L0_conv_bn_beta, L0_conv_bn_mean, L0_conv_bn_var, L0_ffn_router_w, L0_ffn_W1, L0_ffn_b1, L0_ffn_W2, L0_ffn_b2):
    import jax
    import jax.numpy as jnp

    def _L0_conv_ref(x, qkv_w, agg_dw_w, agg_pw_w, proj_w, bn_gamma, bn_beta, bn_mean, bn_var):
        import jax, jax.numpy as jnp
        import numpy as np
        DIM = 8
        EPS_ATT = 1e-15
        BN_EPS = 1e-05

        def conv2d(x, w, groups=1, padding=0):
            return jax.lax.conv_general_dilated(x, w, window_strides=(1, 1), padding=[(padding, padding), (padding, padding)], dimension_numbers=('NCHW', 'OIHW', 'NCHW'), feature_group_count=groups)
        B, _, H, W = x.shape
        qkv = conv2d(x, qkv_w)
        dw_groups = agg_dw_w.shape[0]
        pw_groups = qkv.shape[1] // agg_pw_w.shape[1]
        agg = conv2d(qkv, agg_dw_w, groups=dw_groups, padding=2)
        agg = conv2d(agg, agg_pw_w, groups=pw_groups)
        ms = jnp.concatenate([qkv, agg], axis=1)
        n_h = ms.shape[1] // (3 * DIM)
        t = ms.reshape(B, n_h, 3 * DIM, H * W).transpose(0, 1, 3, 2)
        q = jax.nn.relu(t[..., :DIM])
        k = jax.nn.relu(t[..., DIM:2 * DIM])
        v = t[..., 2 * DIM:]
        v = jnp.concatenate([v, jnp.ones(v.shape[:-1] + (1,), v.dtype)], axis=-1)
        kv = jnp.einsum('bhnd,bhne->bhde', k, v)
        out = jnp.einsum('bhnd,bhde->bhne', q, kv)
        out = out[..., :-1] / (out[..., -1:] + EPS_ATT)
        out = out.transpose(0, 1, 3, 2).reshape(B, n_h * DIM, H, W)
        out = conv2d(out, proj_w)
        inv = jax.lax.rsqrt(bn_var + BN_EPS) * bn_gamma
        out = out * inv[:, None, None] + (bn_beta - bn_mean * inv)[:, None, None]
        return out

    def _L0_ffn_ref(x, router_w, W1, b1, W2, b2):
        import jax, jax.numpy as jnp
        import numpy as np
        N_CONST = 6
        PARTITIONS_OF_6 = [(6,), (5, 1), (4, 2), (4, 1, 1), (3, 3), (3, 2, 1), (3, 1, 1, 1), (2, 2, 2), (2, 2, 1, 1), (2, 1, 1, 1, 1), (1, 1, 1, 1, 1, 1)]
        N_EXPERTS = 6
        TOP_K = 2

        def _partition_weights():
            w = np.zeros((len(PARTITIONS_OF_6), N_EXPERTS), dtype=np.float32)
            for i, partition in enumerate(PARTITIONS_OF_6):
                for j, part in enumerate(partition):
                    if j < N_EXPERTS:
                        w[i, j] = part / N_CONST
            return jnp.asarray(w)
        pw = _partition_weights()
        token_repr = x.mean(axis=1)
        logits = token_repr @ router_w.T
        probs = jax.nn.softmax(logits, axis=-1)
        topk_vals, topk_idx = jax.lax.top_k(probs, TOP_K)
        topk_vals = topk_vals / topk_vals.sum(axis=-1, keepdims=True)
        expert_weights = jnp.einsum('bk,bke->be', topk_vals, pw[topk_idx])
        expert_weights = jnp.where(expert_weights > 1e-06, expert_weights, 0.0)
        h = jax.nn.gelu(jnp.einsum('bsd,edf->ebsf', x, W1) + b1[:, None, None, :], approximate=False)
        out_e = jnp.einsum('ebsf,efd->ebsd', h, W2) + b2[:, None, None, :]
        return jnp.einsum('be,ebsd->bsd', expert_weights, out_e)

    def _gn(v, G=32, eps=1e-05):
        B_, C_, H_, W_ = v.shape
        g = v.reshape(B_, G, C_ // G, H_, W_)
        m = jnp.mean(g, axis=(2, 3, 4), keepdims=True)
        s = jnp.var(g, axis=(2, 3, 4), keepdims=True)
        return ((g - m) / jnp.sqrt(s + eps)).reshape(v.shape)

    def _ln_c(v, eps=1e-06):
        m = jnp.mean(v, axis=1, keepdims=True)
        s = jnp.var(v, axis=1, keepdims=True)
        return (v - m) / jnp.sqrt(s + eps)

    def _ln_t(v, eps=1e-05):
        m = jnp.mean(v, axis=-1, keepdims=True)
        s = jnp.var(v, axis=-1, keepdims=True)
        return (v - m) / jnp.sqrt(s + eps)

    def _to_tokens(v):
        B_, C_, H_, W_ = v.shape
        return v.reshape(B_, C_, H_ * W_).transpose(0, 2, 1)

    def _from_tokens(t, like):
        B_, C_, H_, W_ = like.shape
        return t.transpose(0, 2, 1).reshape(B_, C_, H_, W_)
    x = x + _L0_conv_ref(_ln_c(x), L0_conv_qkv_w, L0_conv_agg_dw_w, L0_conv_agg_pw_w, L0_conv_proj_w, L0_conv_bn_gamma, L0_conv_bn_beta, L0_conv_bn_mean, L0_conv_bn_var)
    t = _to_tokens(x)
    t = t + _L0_ffn_ref(_ln_t(t), L0_ffn_router_w, L0_ffn_W1, L0_ffn_b1, L0_ffn_W2, L0_ffn_b2)
    x = _from_tokens(t, x)
    return x

_drawn_inputs = setup_inputs


def setup_inputs(seed=0):
    import zlib

    import numpy as np

    out = dict(_drawn_inputs(seed))
    spreads = {'L0_conv_bn_gamma': (1.0, 0.6), 'L0_conv_bn_beta': (0.0, 0.1)}
    factors = {'L0_conv_bn_var': 17.264, 'L0_ffn_b1': 8.0, 'L0_ffn_b2': 8.0, 'L0_conv_agg_pw_w': 2.971}
    for name, (base, spread) in spreads.items():
        noise = np.random.default_rng([zlib.crc32(name.encode()), seed]).standard_normal(out[name].shape)
        drawn = base * np.exp(spread * noise) if base else spread * noise
        out[name] = jnp.asarray(drawn.astype(out[name].dtype))
    for name, factor in factors.items():
        out[name] = (out[name] * factor).astype(out[name].dtype)
    return out
```

```python
import numpy as np

from contextlib import ExitStack

import concourse.bass as bass
from concourse import mybir

F32 = mybir.dt.float32
U32 = mybir.dt.uint32
ALU = mybir.AluOpType
ACT = mybir.ActivationFunctionType
AX_X = mybir.AxisListType.X

P = 128
B, C, HH, WW = 8, 256, 32, 32
T = HH * WW
CT = C // P
QKV = 3 * C
QT = QKV // P
DIM = 8
TAPS = 5
E, F = 6, 341
FT = (E * F + P - 1) // P
NP_ = 11
CH = 512
NCH = T // CH
TT = T // P
HG = P // DIM
RD = P + HG
WB = 4
LAG = 2
LN_C_EPS, LN_T_EPS, ATT_EPS, BN_EPS = 1e-6, 1e-5, 1e-15, 1e-5

CENTER = (TAPS // 2) * TAPS + TAPS // 2
TAP_ORDER = [CENTER] + [t for t in range(TAPS * TAPS) if t != CENTER]
PAIR_OPS = 2 * TAPS * TAPS
DW_OPS = QT * TAPS * TAPS


def schedule(has_a, has_c, has_g):
    o = []

    def qkv(*ms):
        if has_a:
            o.extend(("qkv", m, c) for m in ms for c in range(NCH))

    def agg(*ms):
        o.extend(("agg", m, c) for m in ms for c in range(NCH))

    if has_a:
        o.append(("squares", 0))
    if has_c:
        agg(4, 5)
        o.extend(("kv", 1, g) for g in range(2))
    if has_a:
        o.extend(("stats", 0, i) for i in range(2))
        o.extend(("rbc", 0, c) for c in range(NCH))
    if has_c:
        o.extend(("att", 1, t) for t in range(TT))
        o.append(("relu_q",))
    qkv(0, 1)
    if has_c:
        o.extend(("back", 1, c, g) for c in range(NCH) for g in range(2))
        o.append(("proj", 1))
        o.extend(("tok", t) for t in range(TT))
        o.extend(("kv", 0, g) for g in range(2))
    qkv(2, 3)
    if has_c:
        o.extend(("att", 0, t) for t in range(TT))
    qkv(4)
    if has_c:
        o.extend(("back", 0, c, g) for c in range(NCH) for g in range(2))
        o.append(("proj", 0))
        o.append(("squares", 1))
        o.append(("stats", 1, 0))
        o.extend(("rbc", 1, c) for c in range(NCH))
        o.extend([("usum",), ("logits",), ("exp",)])
    qkv(5)
    d = []
    if has_c:
        d = [("ffn", n) for n in range(NCH * FT)]
    if has_g:
        cut = 11 if has_c else 0
        d[cut:cut] = [("agg", m, c) for m in (0, 1) for c in range(NCH)]
        cut = 31 if has_c else len(d)
        d[cut:cut] = [("agg", m, c) for m in (2, 3) for c in range(NCH)]
    return o + d


BANKED = ("qkv", "agg", "kv", "stats", "rbc", "att", "back", "tok", "logits", "ffn")


def fills(order):
    return {it: n for n, it in enumerate([it for it in order if it[0] in BANKED])}


def build(nc, x, w_qkv, w_dw, w_pw, w_proj, bn, bn_rows, w_router, w1, b1, w2, b2, parts, out):
    with ExitStack() as ctx:
        def sb(name, shape, dt=F32):
            return ctx.enter_context(nc.sbuf_tensor(name, shape, dt))

        def sem(name):
            return ctx.enter_context(nc.semaphore(name))

        wq = sb("wq", [P, CT, QKV])
        w1s = sb("w1s", [P, CT, FT * P])
        wp = sb("wp", [P, 2 * CT, C])
        pw = sb("pw", [P, QT, P])
        dww = sb("dww", [P, QT, TAPS * TAPS])
        b1s = sb("b1s", [P, FT])
        b2s = sb("b2s", [P, CT, E])
        rws = sb("rws", [P, CT, NP_])
        pws = sb("pws", [P, FT + E, NP_])
        bnc = sb("bnc", [P, 4, CT])
        ident = sb("ident", [P, P])
        blk = sb("blk", [P, P])
        hm = sb("hm", [P, HG])
        mean_w = sb("mean_w", [P, P])
        ones = sb("ones", [P, P])
        iota11 = sb("iota11", [P, NP_])
        pbias = sb("pbias", [P, CT])
        xa = sb("xa", [P, CT, T])
        xn = sb("xn", [P, CT, T])
        yr = sb("yr", [P, CT, T])
        tn = sb("tn", [P, CT, T])
        rb = [sb(f"rb{i}", [P, T]) for i in range(2)]
        qkvs = [sb(f"qkvs{i}", [P, QT, T]) for i in range(2)]
        dwo = sb("dwo", [P, QT, T])
        qr = sb("qr", [P, 2, T])
        kt = sb("kt", [P, TT, 2, P])
        vt = sb("vt", [P, TT, 2, P + 2])
        ac = sb("ac", [P, 2, T])
        kvr = sb("kvr", [P, 2, P + 1])
        kvm = sb("kvm", [P, 2, RD])
        den = sb("den", [P, TT, 2, HG])
        rden = sb("rden", [P, TT, 2, HG])
        w2s = sb("w2s", [P, FT, C])
        hb = sb("hb", [P, 3, CH])
        st = [sb(f"st{i}", [P, 2, TT]) for i in range(2)]
        sv = [sb(f"sv{i}", [P, 4, TT]) for i in range(2)]
        mhalf = sb("mhalf", [P, TT])
        us = sb("us", [P, CT])
        lg = sb("lg", [P, 16])
        mx = sb("mx", [P, 8])
        ix = sb("ix", [P, 8], U32)
        rt = sb("rt", [P, 16])
        ex = sb("ex", [P, 16])
        wsel = sb("wsel", [P, 2, NP_])
        ewt = sb("ewt", [P, FT + E, NP_])
        ew = sb("ew", [P, 2, FT + E])
        obt = sb("obt", [P, CT, E])
        ob = sb("ob", [P, CT])

        acc = ctx.enter_context(nc.psum_tensor("acc", [P, CT, NCH, CH], F32))
        wbk = [ctx.enter_context(nc.psum_tensor(f"wbk{i}", [P, CH], F32)) for i in range(WB)]

        w_loaded = sem("w_loaded")
        x_loaded = sem("x_loaded")
        yr_loaded = sem("yr_loaded")
        w2_loaded = sem("w2_loaded")
        out_stored = sem("out_stored")
        consts_made = sem("consts_made")
        setup_pool = sem("setup_pool")
        col_means = sem("col_means")
        centred = sem("centred")
        bn_root = sem("bn_root")
        setup_dve = sem("setup_dve")
        bank_filled = sem("bank_filled")
        bank_drained = sem("bank_drained")
        squared = [sem(f"squared{i}") for i in range(2)]
        summed = [sem(f"summed{i}") for i in range(2)]
        ln_chain = [sem(f"ln_chain{i}") for i in range(2)]
        diag_made = [sem(f"diag_made{i}") for i in range(2)]
        normed = [sem(f"normed{i}") for i in range(2)]
        taps = sem("taps")
        kvm_made = sem("kvm_made")
        q_relued = sem("q_relued")
        rden_made = sem("rden_made")
        att_scaled = sem("att_scaled")
        projected = sem("projected")
        y_made = sem("y_made")
        u_made = sem("u_made")
        max_made = sem("max_made")
        exp_made = sem("exp_made")
        route = sem("route")
        w2_scaled = sem("w2_scaled")
        ffn_done = sem("ffn_done")
        out_made = sem("out_made")
        ew_chain = sem("ew_chain")
        pool_gate = sem("pool_gate")
        dve_gate = sem("dve_gate")
        SEED = 2
        ROUTE = 13
        N_W = 11 + HG

        block = ctx.enter_context(nc.Block())

        ORD = {k: schedule(*k) for k in ((1, 0, 0), (1, 0, 1), (1, 1, 1), (0, 1, 1), (0, 1, 0))}
        FIL = {k: fills(o) for k, o in ORD.items()}
        NF = {k: len(f) for k, f in FIL.items()}
        assert all(n % WB == 0 for n in NF.values())
        FULL = (1, 1, 1)
        B1 = NF[1, 0, 0]
        B2 = B1 + NF[1, 0, 1]
        B8 = B2 + (B - 2) * NF[FULL]
        B9 = B8 + NF[0, 1, 1]

        def fill_of_qkv(s_prev_kind, m, c):
            return FIL[s_prev_kind]["qkv", m, c]

        def run_steps(eng, step):
            step((1, 0, 0), 0, 0, 0)
            step((1, 0, 1), 1, 1, B1)
            with eng.Fori(0, (B - 2) // 2) as it:
                step(FULL, it * 2 + 2, 0, it * (2 * NF[FULL]) + B2)
                step(FULL, it * 2 + 3, 1, it * (2 * NF[FULL]) + (B2 + NF[FULL]))
            step((0, 1, 1), B, 0, B8)
            step((0, 1, 0), B + 1, 1, B9)

        @block.sync
        def _(sp):
            for dst, src in ((wq, w_qkv), (wp, w_proj), (w1s, w1)):
                sp.dma_start(dst[:], src.rearrange("(k p) n -> p k n", p=P)).then_inc(w_loaded, 16)
            sp.dma_start(xa[:], x[0].rearrange("(k p) n -> p k n", p=P)).then_inc(x_loaded, 16)
            sp.dma_start(dww[:], w_dw.rearrange("(k p) n -> p k n", p=P)).then_inc(w_loaded, 16)
            sp.dma_start(rws[:], w_router.rearrange("(k p) n -> p k n", p=P)).then_inc(w_loaded, 16)
            sp.dma_start(b2s[:], b2.rearrange("(k p) n -> p k n", p=P)).then_inc(w_loaded, 16)
            sp.dma_start(b1s[:], b1).then_inc(w_loaded, 16)
            sp.dma_start(bnc[:], bn).then_inc(w_loaded, 16)
            sp.dma_start(pws[:], parts.rearrange("p (t n) -> p t n", n=NP_)).then_inc(w_loaded, 16)
            for i in range(2):
                sp.dma_start(tn[:, i, 0:C], bn_rows[i:i + 1, :].to_broadcast([P, C])).then_inc(w_loaded, 16)
            for g in range(HG):
                sp.dma_start(pw[g * DIM:(g + 1) * DIM, :, :], w_pw.rearrange("i (m n) -> i m n", m=QT)
                             ).then_inc(w_loaded, 16)
            sp.dma_start(w2s[:], w2.rearrange("(t p) n -> p t n", p=P)).then_inc(w2_loaded, 16)
            sp.dma_start(yr[:], x[0].rearrange("(k p) n -> p k n", p=P)).then_inc(yr_loaded, 16)

            def load_xa(s):
                sp.wait_ge(normed[0], s * 2)
                sp.dma_start(xa[:], x[bass.ds(s, 1)].rearrange("o (k p) n -> p (o k) n", p=P)
                             ).then_inc(x_loaded, 16)

            def load_w2():
                sp.dma_start(w2s[:], w2.rearrange("(t p) n -> p t n", p=P)).then_inc(w2_loaded, 16)

            def store(j):
                for m in range(CT):
                    sp.wait_ge(out_made, j * CT + (SEED + m + 1))
                    sp.dma_start(out[bass.ds(j, 1), m * P:(m + 1) * P].rearrange("o p n -> p (o n)"),
                                 yr[:, m, :]).then_inc(out_stored, 16)

            def load_yr(j):
                sp.wait_ge(out_stored, j * (16 * CT))
                sp.dma_start(yr[:], x[bass.ds(j, 1)].rearrange("o (k p) n -> p (o k) n", p=P)
                             ).then_inc(yr_loaded, 16)

            load_xa(1)
            with sp.Fori(0, B - 2) as j:
                load_xa(j + 2)
                sp.wait_ge(ffn_done, j + 1)
                load_w2()
                store(j)
                load_yr(j + 1)
            sp.wait_ge(ffn_done, B - 1)
            load_w2()
            store(B - 2)
            load_yr(B - 1)
            store(B - 1)
            sp.wait_ge(out_stored, B * CT * 16)

        @block.tensor
        def _(pe):
            pe.wait_ge(w_loaded, 16 * N_W)
            pe.wait_ge(consts_made, 1)
            af = acc[:].rearrange("p a b n -> p (a b) n")
            for n in range(FT * P // CH):
                for k in range(CT):
                    last = nc.tensor.matmul(af[:, n, :], mean_w[:], w1s[:, k, n * CH:(n + 1) * CH],
                                            start=(k == 0), stop=(k == CT - 1))
            for dst, src in ((wbk[0][:, :], lambda k: wq[:, k, 0:CH]),
                             (wbk[1][:, 0:QKV - CH], lambda k: wq[:, k, CH:QKV]),
                             (wbk[2][:, 0:NP_], lambda k: rws[:, k, :])):
                for k in range(CT):
                    last = nc.tensor.matmul(dst, mean_w[:], src(k), start=(k == 0), stop=(k == CT - 1))
            last.then_inc(col_means, 1)
            pe.wait_ge(centred, 1)

            def step(kind, s, par, base):
                j = s - 2
                cur = qkvs[par]
                n = 0
                for it in ORD[kind]:
                    what = it[0]
                    if what == "proj":
                        h = it[1]
                        for c in range(NCH):
                            for m in range(CT):
                                for g in range(2):
                                    if c == 0 and m == 0 and g == 0:
                                        pe.wait_ge(bank_drained, base + (FIL[kind]["back", h, NCH - 1, 1] + 1))
                                        pe.wait_ge(out_made, j * CT + SEED)
                                    last = nc.tensor.matmul(acc[:, m, c, :], wp[:, 2 * h + g, m * P:(m + 1) * P],
                                                            ac[:, g, c * CH:(c + 1) * CH],
                                                            start=(h == 1 and g == 0), stop=(h == 0 and g == 1),
                                                            skip_group_check=True)
                        if h == 0:
                            last.then_inc(projected, 1)
                        continue
                    if what not in BANKED:
                        continue
                    if not isinstance(base, int) or base + n - (WB - 1) > 0:
                        pe.wait_ge(bank_drained, base + (n - (WB - 1)))
                    b = wbk[n % WB]
                    n += 1
                    if what == "qkv":
                        m, c = it[1:]
                        if m == 0 and c == 0:
                            pe.wait_ge(normed[0], s * 2 + 2)
                        for k in range(CT):
                            last = nc.tensor.matmul(b[:], wq[:, k, m * P:(m + 1) * P], xn[:, k, c * CH:(c + 1) * CH],
                                                    start=(k == 0), stop=(k == CT - 1))
                    elif what == "agg":
                        m, c = it[1:]
                        jj = s - 2 if m >= 4 else s - 1
                        if c == 0 and m % 2 == 0:
                            pe.wait_ge(taps, jj * DW_OPS + (m // 2 + 1) * PAIR_OPS)
                        if m < 2:
                            last = nc.tensor.matmul(b[:], pw[:, m, :], dwo[:, m, c * CH:(c + 1) * CH],
                                                    start=True, stop=True)
                        else:
                            for i in range(CH // P):
                                o = c * CH + i * P
                                last = nc.tensor.matmul(b[:, i * P:(i + 1) * P], dwo[:, m, o:o + P], pw[:, m, :],
                                                        start=True, stop=True)
                    elif what == "tok":
                        t = it[1]
                        for i in range(4):
                            last = nc.tensor.transpose(b[:, i * P:(i + 1) * P], cur[:, 2 + i, t * P:(t + 1) * P],
                                                       ident[:])
                    elif what == "kv":
                        h, g = it[1:]
                        if g == 0:
                            src = ("agg", 5, NCH - 1) if h else ("tok", TT - 1)
                            pe.wait_ge(bank_drained, base + (FIL[kind][src] + 1))
                        for t in range(TT):
                            last = nc.tensor.matmul(b[:, 0:P + 1], kt[:, t, g, :], vt[:, t, g, 0:P + 1],
                                                    start=(t == 0), stop=(t == TT - 1))
                    elif what == "att":
                        h, t = it[1:]
                        if t == 0:
                            pe.wait_ge(kvm_made, j * 8 + (4 if h else 8))
                            if h == 0:
                                pe.wait_ge(q_relued, j * 2 + 2)
                        for g in range(2):
                            last = nc.tensor.matmul(b[:, g * RD:(g + 1) * RD], qr[:, g, t * P:(t + 1) * P],
                                                    kvm[:, g, :], start=True, stop=True)
                    elif what == "back":
                        h, c, g = it[1:]
                        if g == 0:
                            pe.wait_ge(att_scaled, j * 4 + ((0 if h else 2) + c + 1))
                        for i in range(CH // P):
                            last = nc.tensor.transpose(b[:, i * P:(i + 1) * P], kt[:, c * (CH // P) + i, g, :],
                                                       ident[:])
                    elif what == "stats":
                        L, i = it[1:]
                        jj = s if L == 0 else j
                        src = (0,) if (L == 0 and i == 0) else (1,) if L == 0 else (0, 1)
                        for q in src:
                            pe.wait_ge(summed[L], jj * 2 + (q + 1))
                            data = rb[L][:, :] if q == 0 else (xn if L == 0 else tn)[:, 0, :]
                            for t in range(TT):
                                last = nc.tensor.matmul(b[:, q * TT + t:q * TT + t + 1], data[:, t * P:(t + 1) * P],
                                                        mean_w[:, 0:1], start=True, stop=True)
                    elif what == "rbc":
                        L, c = it[1:]
                        if c == 0:
                            pe.wait_ge(diag_made[L], (s if L == 0 else j) + 1)
                        last = nc.tensor.matmul(b[:], ones[:], rb[L][:, c * CH:(c + 1) * CH], start=True, stop=True)
                    elif what == "logits":
                        pe.wait_ge(u_made, j * 2 + (SEED + 2))
                        for k in range(CT):
                            last = nc.tensor.matmul(b[:, 0:NP_], us[:, k:k + 1].to_broadcast([P, P]), rws[:, k, :],
                                                    start=(k == 0), stop=(k == CT - 1))
                    elif what == "ffn":
                        f = it[1]
                        c, t = f // FT, f % FT
                        if f == 0:
                            pe.wait_ge(normed[1], j * 2 + 2)
                        for k in range(CT):
                            last = nc.tensor.matmul(b[:], w1s[:, k, t * P:(t + 1) * P], tn[:, k, c * CH:(c + 1) * CH],
                                                    start=(k == 0), stop=(k == CT - 1))
                    last.then_inc(bank_filled, 1)
                    if what == "ffn" and it[1] >= LAG:
                        last = second(kind, j, base, it[1] - LAG)
                if kind[1]:
                    for f in range(NCH * FT - LAG, NCH * FT):
                        last = second(kind, j, base, f)
                    last.then_inc(ffn_done, 1)

            def second(kind, j, base, f):
                c, t = f // FT, f % FT
                pe.wait_ge(bank_drained, base + (FIL[kind]["ffn", f] + 1))
                if c == 0:
                    pe.wait_ge(w2_scaled, j * FT + (t + 1))
                if f == 0:
                    pe.wait_ge(y_made, j * 2 + 2)
                for m in range(CT):
                    last = nc.tensor.matmul(acc[:, m, c, :], w2s[:, t, m * P:(m + 1) * P], hb[:, f % 3, :],
                                            start=(t == 0), stop=(t == FT - 1), skip_group_check=True)
                return last

            run_steps(pe, step)

        @block.scalar
        def _(act):
            act.wait_ge(w_loaded, 16 * N_W)
            act.wait_ge(setup_dve, 2)
            nc.scalar.activation(tn[:, 1, 0:C], tn[:, 1, 0:C], ACT.Sqrt).then_inc(bn_root, 1)
            nc.scalar.activation(bnc[:, 3, :], bnc[:, 3, :], ACT.Sqrt).then_inc(bn_root, 1)
            act.wait_ge(consts_made, 1)
            act.wait_ge(centred, 1)
            act.sem_inc(u_made, SEED)

            def step(kind, s, par, base):
                j = s - 2
                n = 0
                for it in ORD[kind]:
                    what = it[0]
                    if what == "squares":
                        L = it[1]
                        if L == 0:
                            act.wait_ge(x_loaded, s * 16 + 16)
                        for m in range(CT):
                            if L == 1:
                                act.wait_ge(y_made, j * 2 + (m + 1))
                            src, dst = ((xa, xn), (yr, tn))[L]
                            nc.scalar.activation(dst[:, m, :], src[:, m, :], ACT.Square).then_inc(squared[L], 1)
                        continue
                    if what == "relu_q":
                        for g in range(2):
                            nc.scalar.activation(qr[:, g, :], qkvs[par][:, g, :], ACT.Relu).then_inc(q_relued, 1)
                        continue
                    if what == "usum":
                        for m in range(CT):
                            act.wait_ge(normed[1], j * 2 + 2)
                            if m:
                                act.wait_ge(u_made, j * 2 + (SEED + m))
                            nc.scalar.activation(rb[1][:, :], tn[:, m, :], ACT.Copy, scale=1.0 / T,
                                                 accum_out=us[:, m:m + 1]).then_inc(u_made, 1)
                        continue
                    if what == "exp":
                        act.wait_ge(max_made, j + 1)
                        nc.scalar.activation(ex[:, 0:NP_], lg[:, 0:NP_], ACT.Exp, bias=rt[:, 0:1],
                                             accum_out=rt[:, 1:2]).then_inc(exp_made, 1)
                        nc.scalar.activation(rt[:, 2:4], mx[:, 0:2], ACT.Exp, bias=rt[:, 0:1]).then_inc(exp_made, 1)
                        continue
                    if what not in BANKED:
                        continue
                    act.wait_ge(bank_filled, base + (n + 1))
                    b = wbk[n % WB]
                    n += 1
                    if what == "qkv":
                        m, c = it[1:]
                        if m == 0 and c == 0 and (not isinstance(s, int) or s >= 2):
                            act.wait_ge(taps, s * DW_OPS - DW_OPS)
                            act.wait_ge(q_relued, j * 2 + 2)
                        last = nc.scalar.activation(qkvs[par][:, m, c * CH:(c + 1) * CH], b[:], ACT.Copy)
                    elif what == "agg":
                        m, c = it[1:]
                        tl = slice(c * (CH // P), (c + 1) * (CH // P))
                        bt = b[:].rearrange("p (t n) -> p t n", n=P)
                        if m < 2:
                            last = nc.scalar.activation(qr[:, m, c * CH:(c + 1) * CH], b[:], ACT.Relu)
                        elif m < 4:
                            last = nc.scalar.activation(kt[:, tl, m - 2, :], bt, ACT.Relu)
                        else:
                            last = nc.scalar.activation(vt[:, tl, m - 4, 0:P], bt, ACT.Copy)
                    elif what == "tok":
                        t = it[1]
                        bt = b[:].rearrange("p (a g n) -> p a g n", a=2, g=2)
                        nc.scalar.activation(kt[:, t, :, :], bt[:, 0], ACT.Relu)
                        last = nc.scalar.activation(vt[:, t, :, 0:P], bt[:, 1], ACT.Copy)
                    elif what == "kv":
                        last = nc.scalar.activation(kvr[:, it[2], :], b[:, 0:P + 1], ACT.Copy)
                    elif what == "att":
                        t = it[2]
                        bt = b[:, 0:2 * RD].rearrange("p (g n) -> p g n", g=2)
                        nc.scalar.activation(kt[:, t, :, :], bt[:, :, 0:P], ACT.Copy)
                        last = nc.scalar.activation(den[:, t, :, :], bt[:, :, P:RD], ACT.Copy, bias=ATT_EPS)
                    elif what == "back":
                        h, c, g = it[1:]
                        last = nc.scalar.activation(ac[:, g, c * CH:(c + 1) * CH], b[:], ACT.Copy)
                    elif what == "stats":
                        L, i = it[1:]
                        if L == 0:
                            last = nc.scalar.activation(st[0][:, i, :], b[:, i * TT:(i + 1) * TT], ACT.Copy)
                        else:
                            last = nc.scalar.activation(st[1][:].rearrange("p a b -> p (a b)"), b[:, 0:2 * TT], ACT.Copy)
                    elif what == "rbc":
                        L, c = it[1:]
                        last = nc.scalar.activation(rb[L][:, c * CH:(c + 1) * CH], b[:], ACT.Copy)
                    elif what == "logits":
                        last = nc.scalar.activation(lg[:, 0:NP_], b[:, 0:NP_], ACT.Copy)
                    elif what == "ffn":
                        f = it[1]
                        last = nc.scalar.activation(hb[:, f % 3, :], b[:], ACT.Gelu, bias=b1s[:, f % FT:f % FT + 1])
                    last.then_inc(bank_drained, 1)

            run_steps(act, step)

        @block.gpsimd
        def _(pool):
            chain = [0]

            def after(ins):
                chain[0] += 1
                ins.then_inc(setup_pool, 1)
                pool.wait_ge(setup_pool, chain[0])

            after(nc.gpsimd.memset(ident[:], 0.0))
            after(nc.gpsimd.affine_select(out=ident[:], in_=ident[:], compare_op=ALU.not_equal, fill=1.0, base=0,
                                          pattern=[[-1, P]], channel_multiplier=1))
            for tile, w in ((blk[:].rearrange("p (h i) -> p h i", i=DIM), DIM), (hm[:].unsqueeze(2), 1)):
                after(nc.gpsimd.memset(tile, 1.0))
                after(nc.gpsimd.affine_select(out=tile, in_=tile, compare_op=ALU.is_ge, fill=0.0, base=0,
                                              pattern=[[-DIM, HG], [0, w]], channel_multiplier=1))
                after(nc.gpsimd.affine_select(out=tile, in_=tile, compare_op=ALU.is_ge, fill=0.0, base=DIM - 1,
                                              pattern=[[DIM, HG], [0, w]], channel_multiplier=-1))
            after(nc.gpsimd.memset(mean_w[:], 1.0 / C))
            after(nc.gpsimd.memset(ones[:], 1.0))
            after(nc.gpsimd.memset(mhalf[:], -0.5))
            after(nc.gpsimd.memset(lg[:], -3.0e38))
            after(nc.gpsimd.memset(vt[:, :, :, P:P + 2], 1.0))
            after(nc.gpsimd.iota(iota11[:], pattern=[[1, NP_]], base=0, channel_multiplier=0,
                                 allow_small_or_imprecise_dtypes=True))
            nc.gpsimd.memset(ex[:], 0.0).then_inc(consts_made, 1)
            pool.wait_ge(centred, 1)

            def norm_sums(L, jj, src, dst, kind, base):
                if L == 0:
                    pool.wait_ge(x_loaded, jj * 16 + 16)
                else:
                    pool.wait_ge(y_made, jj * 2 + 2)
                    pool.wait_ge(u_made, jj * 2 + SEED)
                if L == 0:
                    pool.wait_ge(normed[0], jj * 2)
                nc.gpsimd.tensor_tensor(rb[L][:, :], src[:, 0, :], src[:, 1, :], ALU.add).then_inc(summed[L], 1)
                pool.wait_ge(squared[L], jj * 2 + 2)
                nc.gpsimd.tensor_tensor(dst[:, 0, :], dst[:, 0, :], dst[:, 1, :], ALU.add).then_inc(summed[L], 1)

            def norm_scale(L, jj, eps, kind, base):
                pool.wait_ge(bank_drained, base + (FIL[kind]["stats", L, 1 - L] + 1))
                m, q = st[L][:, 0, :], st[L][:, 1, :]
                nc.gpsimd.tensor_tensor(sv[L][:, 0, :], m, m, ALU.mult).then_inc(ln_chain[L], 1)
                pool.wait_ge(ln_chain[L], jj * 4 + 1)
                nc.gpsimd.tensor_tensor(sv[L][:, 1, :], q, sv[L][:, 0, :], ALU.subtract).then_inc(ln_chain[L], 1)
                pool.wait_ge(ln_chain[L], jj * 4 + 2)
                pool.sem_inc(pool_gate, 1)
                nc.gpsimd.tensor_scalar(sv[L][:, 2, :], sv[L][:, 1, :], 1.0, eps, ALU.mult, ALU.add
                                        ).then_inc(ln_chain[L], 1)
                pool.wait_ge(ln_chain[L], jj * 4 + 3)
                nc.gpsimd.tensor_tensor(sv[L][:, 3, :], sv[L][:, 2, :], mhalf[:], ALU.pow).then_inc(ln_chain[L], 1)
                pool.wait_ge(ln_chain[L], jj * 4 + 4)
                nc.gpsimd.tensor_tensor(rb[L][:].rearrange("p (t n) -> p t n", n=P),
                                        ident[:].unsqueeze(1).to_broadcast([P, TT, P]),
                                        sv[L][:, 3, :].unsqueeze(2).to_broadcast([P, TT, P]),
                                        ALU.mult).then_inc(diag_made[L], 1)

            def norm_apply(L, src, dst, kind, base):
                pool.wait_ge(bank_drained, base + (FIL[kind]["rbc", L, NCH - 1] + 1))
                for m in range(CT):
                    nc.gpsimd.tensor_tensor(dst[:, m, :], src[:, m, :], rb[L][:, :], ALU.mult).then_inc(normed[L], 1)

            def mask_kv(h, kind, base):
                pool.wait_ge(bank_drained, base + (FIL[kind]["kv", h, 1] + 1))
                pool.sem_inc(pool_gate, 1)
                for g in range(2):
                    nc.gpsimd.tensor_tensor(kvm[:, g, 0:P], kvr[:, g, 0:P], blk[:], ALU.mult).then_inc(kvm_made, 1)
                    nc.gpsimd.tensor_scalar(kvm[:, g, P:RD], hm[:], kvr[:, g, P:P + 1], 0.0, ALU.mult, ALU.add
                                            ).then_inc(kvm_made, 1)

            def scale_att(h, j):
                for c in range(NCH):
                    pool.wait_ge(rden_made, j * 4 + ((0 if h else 2) + c + 1))
                    tl = slice(c * (CH // P), (c + 1) * (CH // P))
                    v = kt[:, tl].rearrange("p t g (h i) -> p (t g h) i", i=DIM)
                    r = rden[:, tl].rearrange("p t g h -> p (t g h)").unsqueeze(2).to_broadcast([P, CH // P * 2 * HG, DIM])
                    nc.gpsimd.tensor_tensor(v, v, r, ALU.mult).then_inc(att_scaled, 1)

            def step(kind, s, par, base):
                has_a, has_c, _ = kind
                j = s - 2
                if has_a:
                    norm_sums(0, s, xa, xn, kind, base)
                if has_c:
                    mask_kv(1, kind, base)
                if has_a:
                    norm_scale(0, s, LN_C_EPS, kind, base)
                    norm_apply(0, xa, xn, kind, base)
                if has_c:
                    scale_att(1, j)
                    mask_kv(0, kind, base)
                    scale_att(0, j)
                    norm_sums(1, j, yr, tn, kind, base)
                    norm_scale(1, j, LN_T_EPS, kind, base)
                    norm_apply(1, yr, tn, kind, base)
                    pool.wait_ge(w2_loaded, j * 16 + 16)
                    pool.wait_ge(route, j * ROUTE + 10)
                    pool.sem_inc(pool_gate, 1)
                    for t in range(FT):
                        nc.gpsimd.tensor_scalar(w2s[:, t, :], w2s[:, t, :], ew[:, 1, t:t + 1], 0.0, ALU.mult, ALU.add
                                                ).then_inc(w2_scaled, 1)

            run_steps(pool, step)

        @block.vector
        def _(dve):
            dve.wait_ge(w_loaded, 16 * N_W)
            nc.vector.tensor_scalar(tn[:, 1, 0:C], tn[:, 1, 0:C], BN_EPS, None, ALU.add).then_inc(setup_dve, 1)
            nc.vector.tensor_scalar(bnc[:, 3, :], bnc[:, 3, :], BN_EPS, None, ALU.add).then_inc(setup_dve, 1)
            dve.wait_ge(consts_made, 1)
            nc.vector.tensor_tensor(pw[:], pw[:], blk[:].unsqueeze(1).to_broadcast([P, QT, P]), ALU.mult
                                    ).then_inc(setup_dve, 1)
            dve.wait_ge(bn_root, 2)
            nc.vector.reciprocal(tn[:, 1, 0:C], tn[:, 1, 0:C]).then_inc(setup_dve, 1)
            nc.vector.reciprocal(bnc[:, 3, :], bnc[:, 3, :]).then_inc(setup_dve, 1)
            dve.wait_ge(setup_dve, 5)
            nc.vector.tensor_tensor(tn[:, 0, 0:C], tn[:, 0, 0:C], tn[:, 1, 0:C], ALU.mult).then_inc(setup_dve, 1)
            nc.vector.tensor_tensor(bnc[:, 0, :], bnc[:, 0, :], bnc[:, 3, :], ALU.mult).then_inc(setup_dve, 1)
            dve.wait_ge(setup_dve, 7)
            nc.vector.tensor_tensor(bnc[:, 2, :], bnc[:, 2, :], bnc[:, 0, :], ALU.mult).then_inc(setup_dve, 1)
            nc.vector.tensor_tensor(wp[:], wp[:], tn[:, 0, 0:C].unsqueeze(1).to_broadcast([P, 2 * CT, C]), ALU.mult
                                    ).then_inc(setup_dve, 1)
            dve.wait_ge(setup_dve, 8)
            nc.vector.tensor_tensor(pbias[:], bnc[:, 1, :], bnc[:, 2, :], ALU.subtract).then_inc(setup_dve, 1)
            dve.wait_ge(col_means, 1)
            af = acc[:].rearrange("p a b n -> p (a b n)")
            for k in range(CT):
                nc.vector.tensor_tensor(w1s[:, k, :], w1s[:, k, :], af, ALU.subtract).then_inc(setup_dve, 1)
                nc.vector.tensor_tensor(wq[:, k, 0:CH], wq[:, k, 0:CH], wbk[0][:], ALU.subtract).then_inc(setup_dve, 1)
                nc.vector.tensor_tensor(wq[:, k, CH:QKV], wq[:, k, CH:QKV], wbk[1][:, 0:QKV - CH], ALU.subtract
                                        ).then_inc(setup_dve, 1)
                nc.vector.tensor_tensor(rws[:, k, :], rws[:, k, :], wbk[2][:, 0:NP_], ALU.subtract
                                        ).then_inc(setup_dve, 1)
            dve.wait_ge(setup_dve, 10 + 4 * CT)
            nc.vector.memset(rt[:], 0.0).then_inc(centred, 1)
            dve.sem_inc(out_made, SEED)

            def rden_task(h, c, j, kind, base):
                dve.wait_ge(bank_drained, base + (FIL[kind]["att", h, (c + 1) * (CH // P) - 1] + 1))
                tl = slice(c * (CH // P), (c + 1) * (CH // P))
                nc.vector.reciprocal(rden[:, tl], den[:, tl]).then_inc(rden_made, 1)

            def y_task(j):
                dve.wait_ge(projected, j + 1)
                dve.wait_ge(yr_loaded, j * 16 + 16)
                for m in range(CT):
                    nc.vector.scalar_tensor_tensor(out=yr[:, m, :], in0=acc[:, m].rearrange("p c n -> p (c n)"),
                                                   scalar=pbias[:, m:m + 1], in1=yr[:, m, :],
                                                   op0=ALU.add, op1=ALU.add).then_inc(y_made, 1)

            def max_task(j, kind, base):
                dve.wait_ge(bank_drained, base + (FIL[kind]["logits",] + 1))
                dve.sem_inc(dve_gate, 1)
                nc.vector.max(mx[:], lg[:]).then_inc(route, 1)
                dve.wait_ge(route, j * ROUTE + 1)
                dve.sem_inc(dve_gate, 1)
                nc.vector.max_index(ix[:], mx[:], lg[:]).then_inc(route, 1)
                nc.vector.tensor_scalar(rt[:, 0:1], mx[:, 0:1], -1.0, None, ALU.mult).then_inc(max_made, 1)

            def route_task(j):
                dve.wait_ge(exp_made, j * 2 + 2)
                nc.vector.reciprocal(rt[:, 4:5], rt[:, 1:2]).then_inc(route, 1)
                dve.wait_ge(route, j * ROUTE + 3)
                nc.vector.tensor_scalar(rt[:, 6:8], rt[:, 2:4], rt[:, 4:5], None, ALU.mult, ALU.add,
                                        accum_out=rt[:, 8:9]).then_inc(route, 1)
                nc.vector.tensor_copy(rt[:, 12:14], ix[:, 0:2]).then_inc(route, 1)
                dve.wait_ge(route, j * ROUTE + 5)
                nc.vector.reciprocal(rt[:, 9:10], rt[:, 8:9]).then_inc(route, 1)
                dve.wait_ge(route, j * ROUTE + 6)
                nc.vector.tensor_scalar(rt[:, 10:12], rt[:, 6:8], rt[:, 9:10], None, ALU.mult).then_inc(route, 1)
                dve.wait_ge(route, j * ROUTE + 7)
                for i in range(2):
                    ins = nc.vector.tensor_scalar(wsel[:, i, :], iota11[:], rt[:, 12 + i:13 + i], rt[:, 10 + i:11 + i],
                                                  ALU.is_equal, ALU.mult)
                ins.then_inc(route, 1)
                dve.wait_ge(route, j * ROUTE + 8)
                nc.vector.tensor_tensor(wsel[:, 0, :], wsel[:, 0, :], wsel[:, 1, :], ALU.add).then_inc(route, 1)
                dve.wait_ge(route, j * ROUTE + 9)

            def ew_task(j):
                nc.vector.tensor_tensor(ewt[:], pws[:], wsel[:, 0, :].unsqueeze(1).to_broadcast([P, FT + E, NP_]),
                                        ALU.mult).then_inc(ew_chain, 1)
                dve.wait_ge(ew_chain, j * 2 + 1)
                nc.vector.reduce_sum(ew[:, 0, :], ewt[:], axis=AX_X).then_inc(ew_chain, 1)
                dve.wait_ge(ew_chain, j * 2 + 2)
                nc.vector.scalar_tensor_tensor(out=ew[:, 1, :], in0=ew[:, 0, :], scalar=1e-6, in1=ew[:, 0, :],
                                               op0=ALU.is_gt, op1=ALU.mult).then_inc(route, 1)
                dve.wait_ge(route, j * ROUTE + 10)
                nc.vector.tensor_tensor(obt[:], b2s[:], ew[:, 1, FT:FT + E].unsqueeze(1).to_broadcast([P, CT, E]),
                                        ALU.mult).then_inc(route, 1)
                dve.wait_ge(route, j * ROUTE + 11)
                nc.vector.reduce_sum(ob[:], obt[:], axis=AX_X).then_inc(route, 1)
                dve.wait_ge(route, j * ROUTE + 12)
                nc.vector.tensor_copy(rt[:, 14:15], rt[:, 8:9]).then_inc(route, 1)

            def final_task(j):
                dve.wait_ge(ffn_done, j + 1)
                dve.wait_ge(route, j * ROUTE + 13)
                for m in range(CT):
                    nc.vector.scalar_tensor_tensor(out=yr[:, m, :], in0=acc[:, m].rearrange("p c n -> p (c n)"),
                                                   scalar=ob[:, m:m + 1], in1=yr[:, m, :],
                                                   op0=ALU.add, op1=ALU.add).then_inc(out_made, 1)

            TASKS = {30: lambda *a: rden_task(1, 0, *a), 33: lambda *a: rden_task(1, 1, *a),
                     56: lambda *a: rden_task(0, 0, *a), 59: lambda *a: rden_task(0, 1, *a),
                     68: lambda j, k, b: y_task(j), 98: lambda j, k, b: max_task(j, k, b),
                     104: lambda j, k, b: (route_task(j), ew_task(j))}

            def step(kind, s, par, base):
                has_a, has_c, has_g = kind
                j = s - 2
                src = qkvs[1 - par]
                has_dw = has_g
                if not has_dw:
                    if has_c:
                        for t in sorted(TASKS):
                            TASKS[t](j, kind, base)
                        final_task(j)
                    return
                d = (s - 1) * DW_OPS
                prev_end = base
                n = 0
                for pair in range(QT // 2):
                    for i, tap in enumerate(TAP_ORDER):
                        dy, dx = tap // TAPS - TAPS // 2, tap % TAPS - TAPS // 2
                        oy, iy, ny = max(0, -dy), max(0, dy), HH - abs(dy)
                        ox, ixx, nx = max(0, -dx), max(0, dx), WW - abs(dx)
                        for m in (2 * pair, 2 * pair + 1):
                            if has_c and n in TASKS:
                                TASKS[n](j, kind, base)
                            o3 = dwo[:, m, :].rearrange("p (y x) -> p y x", x=WW)
                            i3 = src[:, m, :].rearrange("p (y x) -> p y x", x=WW)
                            w = dww[:, m, tap:tap + 1]
                            if i == 0:
                                if n == 0:
                                    dve.wait_ge(bank_drained, prev_end)
                                if has_c and m % 2 == 0:
                                    if pair < 2:
                                        dve.wait_ge(bank_filled, prev_end)
                                    else:
                                        dve.wait_ge(bank_filled, base + (FIL[kind]["agg", 5, NCH - 1] + 1))
                                nc.vector.tensor_scalar(dwo[:, m, :], src[:, m, :], w, None, ALU.mult
                                                        ).then_inc(taps, 1)
                            else:
                                dve.wait_ge(taps, d + (n - 1))
                                nc.vector.scalar_tensor_tensor(
                                    out=o3[:, oy:oy + ny, ox:ox + nx], in0=i3[:, iy:iy + ny, ixx:ixx + nx], scalar=w,
                                    in1=o3[:, oy:oy + ny, ox:ox + nx], op0=ALU.mult, op1=ALU.add).then_inc(taps, 1)
                            n += 1
                if has_c:
                    final_task(j)

            run_steps(dve, step)


def partition_table():
    partitions = [(6,), (5, 1), (4, 2), (4, 1, 1), (3, 3), (3, 2, 1), (3, 1, 1, 1), (2, 2, 2), (2, 2, 1, 1),
                  (2, 1, 1, 1, 1), (1, 1, 1, 1, 1, 1)]
    w = np.zeros((NP_, E), np.float32)
    for i, part in enumerate(partitions):
        for k, size in enumerate(part):
            w[i, k] = size / 6
    table = np.zeros((P, FT + E, NP_), np.float32)
    for t in range(FT):
        for p in range(P):
            f = t * P + p
            if f < E * F:
                table[p, t] = w[:, f // F]
    table[:, FT:] = w.T[None]
    return table.reshape(P, (FT + E) * NP_)


def kernel(x, L0_conv_qkv_w, L0_conv_agg_dw_w, L0_conv_agg_pw_w, L0_conv_proj_w, L0_conv_bn_gamma, L0_conv_bn_beta,
           L0_conv_bn_mean, L0_conv_bn_var, L0_ffn_router_w, L0_ffn_W1, L0_ffn_b1, L0_ffn_W2, L0_ffn_b2):
    import concourse.bacc as bacc
    from concourse.bass_utils import run_bass_kernel_spmd

    def by_part(a):
        a = np.asarray(a)
        return a.reshape(C // DIM, 3, DIM, -1).transpose(1, 0, 2, 3).reshape(QKV, -1)

    w1 = np.zeros((C, FT * P), np.float32)
    w1[:, :E * F] = np.asarray(L0_ffn_W1).transpose(1, 0, 2).reshape(C, E * F)
    b1 = np.zeros((FT * P,), np.float32)
    b1[:E * F] = np.asarray(L0_ffn_b1).reshape(-1)
    w2 = np.zeros((FT * P, C), np.float32)
    w2[:E * F] = np.asarray(L0_ffn_W2).reshape(E * F, C)
    gamma, beta, mean, var = (np.asarray(a) for a in (L0_conv_bn_gamma, L0_conv_bn_beta, L0_conv_bn_mean,
                                                      L0_conv_bn_var))
    arrays = {
        "x": np.asarray(x).reshape(B, C, T),
        "w_qkv": by_part(L0_conv_qkv_w).T,
        "w_dw": by_part(L0_conv_agg_dw_w),
        "w_pw": by_part(L0_conv_agg_pw_w).T,
        "w_proj": np.asarray(L0_conv_proj_w).reshape(C, 2 * C).T,
        "bn": np.stack([gamma, beta, mean, var]).reshape(4, CT, P).transpose(2, 0, 1),
        "bn_rows": np.stack([gamma, var]),
        "w_router": np.asarray(L0_ffn_router_w).T,
        "w1": w1,
        "b1": b1.reshape(FT, P).T,
        "w2": w2,
        "b2": np.asarray(L0_ffn_b2).T,
        "parts": partition_table(),
    }
    arrays = {n: np.ascontiguousarray(a) for n, a in arrays.items()}
    nc = bacc.Bacc("TRN2", target_bir_lowering=False, num_devices=1)
    args = [nc.dram_tensor(n, a.shape, F32, kind="ExternalInput").ap() for n, a in arrays.items()]
    out = nc.dram_tensor("out", (B, C, T), F32, kind="ExternalOutput").ap()
    build(nc, *args, out)
    r = run_bass_kernel_spmd(nc, [arrays], core_ids=[0])
    return np.asarray(r.results[0]["out"]).reshape(B, C, HH, WW)
```

```python
import numpy as np

from contextlib import ExitStack

import concourse.bass as bass
from concourse import mybir

F32 = mybir.dt.float32
U32 = mybir.dt.uint32
ALU = mybir.AluOpType
ACT = mybir.ActivationFunctionType
AX_X = mybir.AxisListType.X

P = 128
B, C, HH, WW = 8, 256, 32, 32
T = HH * WW
CT = C // P
QKV = 3 * C
QT = QKV // P
DIM = 8
TAPS = 5
E, F = 6, 341
FT = (E * F + P - 1) // P
NP_ = 11
CH = 512
NCH = T // CH
TT = T // P
HG = P // DIM
RD = P + HG
WB = 2
RW = 6
AHEAD = 2
LAG = 2
LN_C_EPS, LN_T_EPS, ATT_EPS, BN_EPS = 1e-6, 1e-5, 1e-15, 1e-5

CENTER = (TAPS // 2) * TAPS + TAPS // 2
LAST_TAP = CENTER + 1
TAP_ORDER = [CENTER] + [t for t in range(TAPS * TAPS) if t not in (CENTER, LAST_TAP)] + [LAST_TAP]
PAIR_OPS = 2 * TAPS * TAPS + 2
DW_OPS = QT // 2 * PAIR_OPS


def schedule(a, d, c, f):
    o = []
    features = iter(range(NCH * FT if f else 0))

    def second(n):
        o.append(("second", n))
        if n % FT == FT - 1:
            o.append(("final", n // FT))

    def ffn(k):
        for _, n in zip(range(k), features):
            o.append(("ffn", n))
            if n >= LAG:
                second(n - LAG)

    def qkv(m):
        o.extend(("qkv", m, ch) for ch in range(NCH))

    def agg(*ms):
        o.extend(("agg", m, ch) for m in ms for ch in range(NCH))

    if d:
        qkv(4)
        qkv(5)
    if a:
        o.extend([("squares", 0), ("sums", 0)])
    if c:
        agg(4, 5, 2, 3)
        o.extend([("kv", 1, 0), ("kv", 1, 1), ("mask", 1)])
        agg(0, 1)
    if a:
        o.append(("stats", 0, 0))
    ffn(1)
    if a:
        o.extend([("stats", 0, 1), ("rnorm", 0)])
    if c:
        o.extend(("att", 1, t) for t in range(TT))
        o.append(("scale", 1))
    ffn(3)
    if a:
        o.extend([("rbc", 0, ch) for ch in range(NCH)] + [("apply", 0)])
    if c:
        o.extend(("back", 1, ch, g) for ch in range(NCH) for g in range(2))
        o.extend(("proj", ch, m) for ch in range(NCH) for m in range(CT))
        o.extend([("squares", 1), ("sums", 1)])
    if d:
        o.append(("relu_q",))
        o.extend(("tok", t) for t in range(TT))
        o.extend([("kv", 0, 0), ("kv", 0, 1), ("mask", 0)])
    ffn(2)
    if c:
        o.extend([("stats", 1, 0), ("rnorm", 1)])
    if d:
        o.extend(("att", 0, t) for t in range(TT))
        o.append(("scale", 0))
    ffn(3)
    if c:
        o.extend([("rbc", 1, ch) for ch in range(NCH)] + [("apply", 1)])
    if d:
        o.extend(("back", 0, ch, g) for ch in range(NCH) for g in range(2))
    ffn(2)
    if a:
        qkv(0)
    if c:
        o.append(("usum",))
    if a:
        qkv(1)
    ffn(2)
    if c:
        o.append(("logits",))
    ffn(2)
    if c:
        o.append(("exp",))
    ffn(8)
    if a:
        qkv(2)
    ffn(NCH * FT)
    for ch in range(NCH):
        if a:
            o.append(("qkv", 3, ch))
        if f:
            second(NCH * FT - LAG + ch)
    return o


BANKED = ("qkv", "agg", "kv", "stats", "rbc", "att", "back", "proj", "tok", "logits", "ffn")


def fills(order):
    return {it: n for n, it in enumerate([it for it in order if it[0] in BANKED])}


def past(s, k):
    return not isinstance(s, int) or s >= k


def build(nc, x, w_qkv, w_dw, w_pw, w_proj, bn, bn_rows, w_router, w1, b1, w2, b2, parts, out):
    with ExitStack() as ctx:
        def sb(name, shape, dt=F32):
            return ctx.enter_context(nc.sbuf_tensor(name, shape, dt))

        def sem(name):
            return ctx.enter_context(nc.semaphore(name))

        wq = sb("wq", [P, CT, QKV])
        w1s = sb("w1s", [P, CT, FT * P])
        wp = sb("wp", [P, 2 * CT, C])
        pw = sb("pw", [P, QT, P])
        dww = sb("dww", [P, QT, TAPS * TAPS])
        b1s = sb("b1s", [P, FT])
        b2s = sb("b2s", [P, CT, E])
        rws = sb("rws", [P, CT, NP_])
        pws = sb("pws", [P, FT + E, NP_])
        bnc = sb("bnc", [P, 4, CT])
        ident = sb("ident", [P, P])
        blk = sb("blk", [P, P])
        hm = sb("hm", [P, HG])
        mean_w = sb("mean_w", [P, P])
        ones = sb("ones", [P, P])
        iota11 = sb("iota11", [P, NP_])
        pbias = sb("pbias", [P, CT])
        xa = sb("xa", [P, CT, T])
        xn = sb("xn", [P, CT, T])
        yrs = [sb(f"yr{i}", [P, CT, T]) for i in range(2)]
        tns = [sb(f"tn{i}", [P, CT, T]) for i in range(2)]
        rb = [sb(f"rb{i}", [P, T]) for i in range(2)]
        qkvs = sb("qkvs", [P, QT, T])
        dwo = sb("dwo", [P, QT, T])
        qr = sb("qr", [P, 2, T])
        kt = sb("kt", [P, TT, 2, P])
        vt = sb("vt", [P, TT, 2, P + 2])
        ac = sb("ac", [P, 4, T])
        kvr = sb("kvr", [P, 2, P + 1])
        kvm = sb("kvm", [P, 2, RD])
        den = sb("den", [P, TT, 2, HG])
        rden = sb("rden", [P, TT, 2, HG])
        w2s = sb("w2s", [P, FT, C])
        w2r = sb("w2r", [P, RW, C])
        proj_b = sb("proj_b", [P, 2, CH])
        ffn_b = sb("ffn_b", [P, 2, CH])
        hb = sb("hb", [P, 3, CH])
        st = [sb(f"st{i}", [P, 2, TT]) for i in range(2)]
        sv = [sb(f"sv{i}", [P, 4, TT]) for i in range(2)]
        mhalf = sb("mhalf", [P, TT])
        us = sb("us", [P, CT])
        lg = sb("lg", [P, 16])
        mx = sb("mx", [P, 8])
        ix = sb("ix", [P, 8], U32)
        rt = sb("rt", [P, 16])
        ex = sb("ex", [P, 16])
        wsel = sb("wsel", [P, 2, NP_])
        ewt = sb("ewt", [P, FT + E, NP_])
        ewr = sb("ewr", [P, FT + E])
        ews = [sb(f"ew{i}", [P, FT + E]) for i in range(2)]
        obt = sb("obt", [P, CT, E])
        obs = [sb(f"ob{i}", [P, CT]) for i in range(2)]

        dacc = ctx.enter_context(nc.psum_tensor("dacc", [P, 2, T], F32))
        acc = ctx.enter_context(nc.psum_tensor("acc", [P, CT, CH], F32))
        wbk = [ctx.enter_context(nc.psum_tensor(f"wbk{i}", [P, CH], F32)) for i in range(WB)]

        w_loaded = sem("w_loaded")
        x_loaded = sem("x_loaded")
        yr_loaded = sem("yr_loaded")
        w2_loaded = sem("w2_loaded")
        out_stored = sem("out_stored")
        consts_made = sem("consts_made")
        setup_pool = sem("setup_pool")
        col_means = sem("col_means")
        centred = sem("centred")
        bn_root = sem("bn_root")
        setup_dve = sem("setup_dve")
        bank_filled = sem("bank_filled")
        bank_drained = sem("bank_drained")
        squared = [sem(f"squared{i}") for i in range(2)]
        summed = [sem(f"summed{i}") for i in range(2)]
        ln_chain = [sem(f"ln_chain{i}") for i in range(2)]
        diag_made = [sem(f"diag_made{i}") for i in range(2)]
        normed = [sem(f"normed{i}") for i in range(2)]
        taps = sem("taps")
        kvm_made = [sem(f"kvm_made{i}") for i in range(2)]
        rden_made = [sem(f"rden_made{i}") for i in range(2)]
        att_scaled = [sem(f"att_scaled{i}") for i in range(2)]
        q_relued = sem("q_relued")
        y_made = sem("y_made")
        u_made = sem("u_made")
        max_made = sem("max_made")
        exp_made = sem("exp_made")
        route = sem("route")
        w2_scaled = sem("w2_scaled")
        w2_used = sem("w2_used")
        acc_drained = sem("acc_drained")
        out_made = sem("out_made")
        ew_chain = sem("ew_chain")
        pool_gate = sem("pool_gate")
        dve_gate = sem("dve_gate")
        SEED = 4
        NB = CT * NCH
        ROUTE = 13
        N_W = 11 + HG

        block = ctx.enter_context(nc.Block())

        KINDS = [(1, 0, 0, 0), (1, 1, 0, 0), (1, 1, 1, 0), (1, 1, 1, 1), (0, 1, 1, 1), (0, 0, 1, 1), (0, 0, 0, 1)]
        FULL = KINDS[3]
        ORD = {k: schedule(*k) for k in KINDS}
        FIL = {k: fills(o) for k, o in ORD.items()}
        NF = {k: len(f) for k, f in FIL.items()}
        assert all(n % WB == 0 for n in NF.values()) and B % 2 == 0

        def tail(it):
            return min(NF[k] - (FIL[k][it] + 1) for k in KINDS[:4])

        def run_steps(eng, step):
            base = 0
            for s in range(3):
                step(KINDS[s], s, s % 2, base)
                base += NF[KINDS[s]]
            pairs = (B - 4) // 2
            with eng.Fori(0, pairs) as it:
                step(FULL, it * 2 + 3, 1, it * (2 * NF[FULL]) + base)
                step(FULL, it * 2 + 4, 0, it * (2 * NF[FULL]) + (base + NF[FULL]))
            base += 2 * pairs * NF[FULL]
            for s in range(3 + 2 * pairs, B + 3):
                kind = KINDS[max(3, 4 + s - B)]
                step(kind, s, s % 2, base)
                base += NF[kind]

        @block.sync
        def _(sp):
            for dst, src in ((wq, w_qkv), (wp, w_proj), (w1s, w1)):
                sp.dma_start(dst[:], src.rearrange("(k p) n -> p k n", p=P)).then_inc(w_loaded, 16)
            sp.dma_start(xa[:], x[0].rearrange("(k p) n -> p k n", p=P)).then_inc(x_loaded, 16)
            sp.dma_start(dww[:], w_dw.rearrange("(k p) n -> p k n", p=P)).then_inc(w_loaded, 16)
            sp.dma_start(rws[:], w_router.rearrange("(k p) n -> p k n", p=P)).then_inc(w_loaded, 16)
            sp.dma_start(b2s[:], b2.rearrange("(k p) n -> p k n", p=P)).then_inc(w_loaded, 16)
            sp.dma_start(b1s[:], b1).then_inc(w_loaded, 16)
            sp.dma_start(bnc[:], bn).then_inc(w_loaded, 16)
            sp.dma_start(pws[:], parts.rearrange("p (t n) -> p t n", n=NP_)).then_inc(w_loaded, 16)
            for i in range(2):
                sp.dma_start(tns[0][:, i, 0:C], bn_rows[i:i + 1, :].to_broadcast([P, C])).then_inc(w_loaded, 16)
            for g in range(HG):
                sp.dma_start(pw[g * DIM:(g + 1) * DIM, :, :], w_pw.rearrange("i (m n) -> i m n", m=QT)
                             ).then_inc(w_loaded, 16)
            sp.dma_start(w2s[:], w2.rearrange("(t p) n -> p t n", p=P)).then_inc(w2_loaded, 16)
            for i in range(2):
                sp.dma_start(yrs[i][:], x[i].rearrange("(k p) n -> p k n", p=P)).then_inc(yr_loaded, 16)

            def step(kind, s, par, base):
                if kind[0] and (not isinstance(s, int) or s < B - 1):
                    sp.wait_ge(normed[0], s * 2 + 2)
                    sp.dma_start(xa[:], x[bass.ds(s + 1, 1)].rearrange("o (k p) n -> p (o k) n", p=P)
                                 ).then_inc(x_loaded, 16)
                if kind[3]:
                    jf = s - 3
                    yr = yrs[1 - par]
                    for c in range(NCH):
                        sp.wait_ge(out_made, jf * NB + (SEED + (c + 1) * CT))
                        sp.dma_start(out[bass.ds(jf, 1), :, c * CH:(c + 1) * CH].rearrange("o (k p) n -> p (o k) n", p=P),
                                     yr[:, :, c * CH:(c + 1) * CH]).then_inc(out_stored, 16)
                    if not isinstance(s, int) or s <= B:
                        sp.wait_ge(out_stored, jf * (16 * NCH) + 16 * NCH)
                        sp.dma_start(yr[:], x[bass.ds(s - 1, 1)].rearrange("o (k p) n -> p (o k) n", p=P)
                                     ).then_inc(yr_loaded, 16)

            run_steps(sp, step)
            sp.wait_ge(out_stored, B * NCH * 16)

        @block.tensor
        def _(pe):
            pe.wait_ge(w_loaded, 16 * N_W)
            pe.wait_ge(consts_made, 1)
            af = dacc[:].rearrange("p a (b n) -> p (a b) n", n=CH)
            for n in range(FT * P // CH):
                for k in range(CT):
                    last = nc.tensor.matmul(af[:, n, :], mean_w[:], w1s[:, k, n * CH:(n + 1) * CH],
                                            start=(k == 0), stop=(k == CT - 1))
            for dst, src in ((wbk[0][:, :], lambda k: wq[:, k, 0:CH]),
                             (wbk[1][:, 0:QKV - CH], lambda k: wq[:, k, CH:QKV]),
                             (acc[:, 0, 0:NP_], lambda k: rws[:, k, :])):
                for k in range(CT):
                    last = nc.tensor.matmul(dst, mean_w[:], src(k), start=(k == 0), stop=(k == CT - 1))
            last.then_inc(col_means, 1)
            pe.wait_ge(centred, 1)
            pe.sem_inc(w2_used, RW)

            def step(kind, s, par, base):
                j = s - 2
                jf = s - 3
                tn = tns[par]
                n = 0
                for it in ORD[kind]:
                    what = it[0]
                    if what == "second":
                        second(kind, jf, base, it[1])
                        continue
                    if what not in BANKED:
                        continue
                    if not isinstance(base, int) or base + n - (WB - 1) > 0:
                        pe.wait_ge(bank_drained, base + (n - (WB - 1)))
                    b = wbk[n % WB]
                    n += 1
                    if what == "qkv":
                        m, c = it[1:]
                        if m == 0 and c == 0:
                            pe.wait_ge(normed[0], s * 2 + 2)
                        for k in range(CT):
                            last = nc.tensor.matmul(b[:], wq[:, k, m * P:(m + 1) * P], xn[:, k, c * CH:(c + 1) * CH],
                                                    start=(k == 0), stop=(k == CT - 1))
                    elif what == "agg":
                        m, c = it[1:]
                        if m == 4 and c == 0:
                            pe.wait_ge(taps, j * DW_OPS + DW_OPS)
                        if m < 2:
                            last = nc.tensor.matmul(b[:], pw[:, m, :], dwo[:, m, c * CH:(c + 1) * CH],
                                                    start=True, stop=True)
                        else:
                            for i in range(CH // P):
                                o = c * CH + i * P
                                last = nc.tensor.matmul(b[:, i * P:(i + 1) * P], dwo[:, m, o:o + P], pw[:, m, :],
                                                        start=True, stop=True)
                    elif what == "tok":
                        t = it[1]
                        if t == 0:
                            pe.wait_ge(bank_drained, base + (FIL[kind]["qkv", 5, NCH - 1] + 1))
                        for i in range(4):
                            last = nc.tensor.transpose(b[:, i * P:(i + 1) * P], qkvs[:, 2 + i, t * P:(t + 1) * P],
                                                       ident[:])
                    elif what == "kv":
                        h, g = it[1:]
                        if g == 0:
                            src = ("agg", 3, NCH - 1) if h else ("tok", TT - 1)
                            pe.wait_ge(bank_drained, base + (FIL[kind][src] + 1))
                        for t in range(TT):
                            last = nc.tensor.matmul(b[:, 0:P + 1], kt[:, t, g, :], vt[:, t, g, 0:P + 1],
                                                    start=(t == 0), stop=(t == TT - 1))
                    elif what == "att":
                        h, t = it[1:]
                        if t == 0:
                            pe.wait_ge(kvm_made[h], (s - 1 - h) * 4 + 4)
                            if h == 0:
                                pe.wait_ge(q_relued, s * 2)
                            else:
                                pe.wait_ge(bank_drained, base + (FIL[kind]["agg", 1, NCH - 1] + 1))
                        for g in range(2):
                            last = nc.tensor.matmul(b[:, g * RD:(g + 1) * RD], qr[:, g, t * P:(t + 1) * P],
                                                    kvm[:, g, :], start=True, stop=True)
                    elif what == "back":
                        h, c, g = it[1:]
                        if g == 0:
                            pe.wait_ge(att_scaled[h], (s - 1 - h) * 2 + (c + 1))
                        for i in range(CH // P):
                            last = nc.tensor.transpose(b[:, i * P:(i + 1) * P], kt[:, c * (CH // P) + i, g, :],
                                                       ident[:])
                    elif what == "proj":
                        c, m = it[1:]
                        if c == 0 and m == 0:
                            pe.wait_ge(bank_drained, base + (FIL[kind]["back", 1, NCH - 1, 1] + 1))
                        for k in range(2 * CT):
                            last = nc.tensor.matmul(b[:], wp[:, k, m * P:(m + 1) * P], ac[:, k, c * CH:(c + 1) * CH],
                                                    start=(k == 0), stop=(k == 2 * CT - 1))
                    elif what == "stats":
                        L, i = it[1:]
                        jj = s if L == 0 else j
                        src = (0,) if (L == 0 and i == 0) else (1,) if L == 0 else (0, 1)
                        for q in src:
                            pe.wait_ge(summed[L], jj * 2 + (q + 1))
                            data = rb[L][:, :] if q == 0 else (xn if L == 0 else tn)[:, 0, :]
                            for t in range(TT):
                                last = nc.tensor.matmul(b[:, q * TT + t:q * TT + t + 1], data[:, t * P:(t + 1) * P],
                                                        mean_w[:, 0:1], start=True, stop=True)
                    elif what == "rbc":
                        L, c = it[1:]
                        if c == 0:
                            pe.wait_ge(diag_made[L], (s if L == 0 else j) + 1)
                        last = nc.tensor.matmul(b[:], ones[:], rb[L][:, c * CH:(c + 1) * CH], start=True, stop=True)
                    elif what == "logits":
                        pe.wait_ge(u_made, j * 2 + 2)
                        for k in range(CT):
                            last = nc.tensor.matmul(b[:, 0:NP_], us[:, k:k + 1].to_broadcast([P, P]), rws[:, k, :],
                                                    start=(k == 0), stop=(k == CT - 1))
                    elif what == "ffn":
                        f = it[1]
                        c, t = f // FT, f % FT
                        if f == 0:
                            pe.wait_ge(normed[1], jf * 2 + 2)
                        for k in range(CT):
                            last = nc.tensor.matmul(b[:], w1s[:, k, t * P:(t + 1) * P],
                                                    tns[1 - par][:, k, c * CH:(c + 1) * CH],
                                                    start=(k == 0), stop=(k == CT - 1))
                    last.then_inc(bank_filled, 1)

            def second(kind, jf, base, f):
                c, t = f // FT, f % FT
                pe.wait_ge(bank_drained, base + (FIL[kind]["ffn", f] + 1))
                pe.wait_ge(w2_scaled, jf * (NCH * FT) + (f + 1))
                if t == 0:
                    pe.wait_ge(acc_drained, jf * NB + (SEED + c * CT))
                for m in range(CT):
                    last = nc.tensor.matmul(acc[:, m, :], w2r[:, f % RW, m * P:(m + 1) * P], hb[:, f % 3, :],
                                            start=(t == 0), stop=(t == FT - 1), skip_group_check=True)
                last.then_inc(w2_used, 1)

            run_steps(pe, step)

        @block.scalar
        def _(act):
            act.wait_ge(w_loaded, 16 * N_W)
            act.wait_ge(setup_dve, 2)
            nc.scalar.activation(tns[0][:, 1, 0:C], tns[0][:, 1, 0:C], ACT.Sqrt).then_inc(bn_root, 1)
            nc.scalar.activation(bnc[:, 3, :], bnc[:, 3, :], ACT.Sqrt).then_inc(bn_root, 1)
            act.wait_ge(consts_made, 1)
            act.wait_ge(centred, 1)
            act.sem_inc(acc_drained, SEED)

            def step(kind, s, par, base):
                j = s - 2
                jf = s - 3
                yr, tn = yrs[par], tns[par]
                n = 0
                for it in ORD[kind]:
                    what = it[0]
                    if what == "squares":
                        L = it[1]
                        if L == 0:
                            act.wait_ge(x_loaded, s * 16 + 16)
                        for m in range(CT):
                            if L == 1:
                                act.wait_ge(y_made, j * NB + NB)
                            src, dst = ((xa, xn), (yr, tn))[L]
                            nc.scalar.activation(dst[:, m, :], src[:, m, :], ACT.Square).then_inc(squared[L], 1)
                        continue
                    if what == "relu_q":
                        for g in range(2):
                            nc.scalar.activation(qr[:, g, :], qkvs[:, g, :], ACT.Relu).then_inc(q_relued, 1)
                        continue
                    if what == "usum":
                        for m in range(CT):
                            act.wait_ge(normed[1], j * 2 + 2)
                            if m:
                                act.wait_ge(u_made, j * 2 + m)
                            nc.scalar.activation(rb[1][:, :], tn[:, m, :], ACT.Copy, scale=1.0 / T,
                                                 accum_out=us[:, m:m + 1]).then_inc(u_made, 1)
                        continue
                    if what == "exp":
                        act.wait_ge(max_made, j + 1)
                        nc.scalar.activation(ex[:, 0:NP_], lg[:, 0:NP_], ACT.Exp, bias=rt[:, 0:1],
                                             accum_out=rt[:, 1:2]).then_inc(exp_made, 1)
                        nc.scalar.activation(rt[:, 2:4], mx[:, 0:2], ACT.Exp, bias=rt[:, 0:1]).then_inc(exp_made, 1)
                        continue
                    if what == "final":
                        c = it[1]
                        if c == 0:
                            act.wait_ge(route, jf * ROUTE + ROUTE)
                        act.wait_ge(w2_used, jf * (NCH * FT) + (RW + (c + 1) * FT))
                        for m in range(CT):
                            act.wait_ge(out_made, jf * NB + (SEED + c * CT + m - 1))
                            nc.scalar.activation(ffn_b[:, m, :], acc[:, m, :], ACT.Identity,
                                                 bias=obs[1 - par][:, m:m + 1]).then_inc(acc_drained, 1)
                        continue
                    if what not in BANKED:
                        continue
                    act.wait_ge(bank_filled, base + (n + 1))
                    b = wbk[n % WB]
                    n += 1
                    if what == "qkv":
                        m, c = it[1:]
                        if c == 0 and m % 2 == 0:
                            if m == 4 and past(s, 2):
                                act.wait_ge(taps, s * DW_OPS - DW_OPS)
                            if m < 4 and past(s, 1):
                                act.wait_ge(taps, s * DW_OPS - DW_OPS + (m // 2 + 1) * PAIR_OPS)
                            if m == 0 and past(s, 1):
                                act.wait_ge(q_relued, s * 2)
                        last = nc.scalar.activation(qkvs[:, m, c * CH:(c + 1) * CH], b[:], ACT.Copy)
                    elif what == "agg":
                        m, c = it[1:]
                        tl = slice(c * (CH // P), (c + 1) * (CH // P))
                        bt = b[:].rearrange("p (t n) -> p t n", n=P)
                        if m < 2:
                            last = nc.scalar.activation(qr[:, m, c * CH:(c + 1) * CH], b[:], ACT.Relu)
                        elif m < 4:
                            last = nc.scalar.activation(kt[:, tl, m - 2, :], bt, ACT.Relu)
                        else:
                            last = nc.scalar.activation(vt[:, tl, m - 4, 0:P], bt, ACT.Copy)
                    elif what == "tok":
                        t = it[1]
                        bt = b[:].rearrange("p (a g n) -> p a g n", a=2, g=2)
                        nc.scalar.activation(kt[:, t, :, :], bt[:, 0], ACT.Relu)
                        last = nc.scalar.activation(vt[:, t, :, 0:P], bt[:, 1], ACT.Copy)
                    elif what == "kv":
                        last = nc.scalar.activation(kvr[:, it[2], :], b[:, 0:P + 1], ACT.Copy)
                    elif what == "att":
                        t = it[2]
                        bt = b[:, 0:2 * RD].rearrange("p (g n) -> p g n", g=2)
                        nc.scalar.activation(kt[:, t, :, :], bt[:, :, 0:P], ACT.Copy)
                        last = nc.scalar.activation(den[:, t, :, :], bt[:, :, P:RD], ACT.Copy, bias=ATT_EPS)
                    elif what == "back":
                        h, c, g = it[1:]
                        last = nc.scalar.activation(ac[:, 2 * h + g, c * CH:(c + 1) * CH], b[:], ACT.Copy)
                    elif what == "proj":
                        c, m = it[1:]
                        if past(s, 3) or c > 0:
                            act.wait_ge(y_made, j * NB + (c * CT + m - 1))
                        last = nc.scalar.activation(proj_b[:, m, :], b[:], ACT.Identity, bias=pbias[:, m:m + 1])
                    elif what == "stats":
                        L, i = it[1:]
                        if L == 0:
                            last = nc.scalar.activation(st[0][:, i, :], b[:, i * TT:(i + 1) * TT], ACT.Copy)
                        else:
                            last = nc.scalar.activation(st[1][:].rearrange("p a b -> p (a b)"), b[:, 0:2 * TT], ACT.Copy)
                    elif what == "rbc":
                        L, c = it[1:]
                        last = nc.scalar.activation(rb[L][:, c * CH:(c + 1) * CH], b[:], ACT.Copy)
                    elif what == "logits":
                        last = nc.scalar.activation(lg[:, 0:NP_], b[:, 0:NP_], ACT.Copy)
                    elif what == "ffn":
                        f = it[1]
                        last = nc.scalar.activation(hb[:, f % 3, :], b[:], ACT.Gelu, bias=b1s[:, f % FT:f % FT + 1])
                    last.then_inc(bank_drained, 1)

            run_steps(act, step)

        @block.gpsimd
        def _(pool):
            chain = [0]

            def after(ins):
                chain[0] += 1
                ins.then_inc(setup_pool, 1)
                pool.wait_ge(setup_pool, chain[0])

            after(nc.gpsimd.memset(ident[:], 0.0))
            after(nc.gpsimd.affine_select(out=ident[:], in_=ident[:], compare_op=ALU.not_equal, fill=1.0, base=0,
                                          pattern=[[-1, P]], channel_multiplier=1))
            for tile, w in ((blk[:].rearrange("p (h i) -> p h i", i=DIM), DIM), (hm[:].unsqueeze(2), 1)):
                after(nc.gpsimd.memset(tile, 1.0))
                after(nc.gpsimd.affine_select(out=tile, in_=tile, compare_op=ALU.is_ge, fill=0.0, base=0,
                                              pattern=[[-DIM, HG], [0, w]], channel_multiplier=1))
                after(nc.gpsimd.affine_select(out=tile, in_=tile, compare_op=ALU.is_ge, fill=0.0, base=DIM - 1,
                                              pattern=[[DIM, HG], [0, w]], channel_multiplier=-1))
            after(nc.gpsimd.memset(mean_w[:], 1.0 / C))
            after(nc.gpsimd.memset(ones[:], 1.0))
            after(nc.gpsimd.memset(mhalf[:], -0.5))
            after(nc.gpsimd.memset(lg[:], -3.0e38))
            after(nc.gpsimd.memset(vt[:, :, :, P:P + 2], 1.0))
            after(nc.gpsimd.iota(iota11[:], pattern=[[1, NP_]], base=0, channel_multiplier=0,
                                 allow_small_or_imprecise_dtypes=True))
            nc.gpsimd.memset(ex[:], 0.0).then_inc(consts_made, 1)
            pool.wait_ge(centred, 1)
            pool.wait_ge(w2_loaded, 16)
            pool.sem_inc(out_made, SEED)

            def norm_sums(L, s, jj, src, dst):
                if L == 0:
                    pool.wait_ge(x_loaded, jj * 16 + 16)
                else:
                    pool.wait_ge(y_made, jj * NB + NB)
                    if past(s, 3):
                        pool.wait_ge(u_made, jj * 2)
                if L == 0 and past(s, 1):
                    pool.wait_ge(normed[0], jj * 2)
                nc.gpsimd.tensor_tensor(rb[L][:, :], src[:, 0, :], src[:, 1, :], ALU.add).then_inc(summed[L], 1)
                pool.wait_ge(squared[L], jj * 2 + 2)
                nc.gpsimd.tensor_tensor(dst[:, 0, :], dst[:, 0, :], dst[:, 1, :], ALU.add).then_inc(summed[L], 1)

            def norm_scale(L, jj, eps, kind, base):
                pool.wait_ge(bank_drained, base + (FIL[kind]["stats", L, 1 - L] + 1))
                m, q = st[L][:, 0, :], st[L][:, 1, :]
                nc.gpsimd.tensor_tensor(sv[L][:, 0, :], m, m, ALU.mult).then_inc(ln_chain[L], 1)
                pool.wait_ge(ln_chain[L], jj * 4 + 1)
                nc.gpsimd.tensor_tensor(sv[L][:, 1, :], q, sv[L][:, 0, :], ALU.subtract).then_inc(ln_chain[L], 1)
                pool.wait_ge(ln_chain[L], jj * 4 + 2)
                pool.sem_inc(pool_gate, 1)
                nc.gpsimd.tensor_scalar(sv[L][:, 2, :], sv[L][:, 1, :], 1.0, eps, ALU.mult, ALU.add
                                        ).then_inc(ln_chain[L], 1)
                pool.wait_ge(ln_chain[L], jj * 4 + 3)
                nc.gpsimd.tensor_tensor(sv[L][:, 3, :], sv[L][:, 2, :], mhalf[:], ALU.pow).then_inc(ln_chain[L], 1)
                pool.wait_ge(ln_chain[L], jj * 4 + 4)
                nc.gpsimd.tensor_tensor(rb[L][:].rearrange("p (t n) -> p t n", n=P),
                                        ident[:].unsqueeze(1).to_broadcast([P, TT, P]),
                                        sv[L][:, 3, :].unsqueeze(2).to_broadcast([P, TT, P]),
                                        ALU.mult).then_inc(diag_made[L], 1)

            def norm_apply(L, src, dst, kind, base):
                pool.wait_ge(bank_drained, base + (FIL[kind]["rbc", L, NCH - 1] + 1))
                for m in range(CT):
                    nc.gpsimd.tensor_tensor(dst[:, m, :], src[:, m, :], rb[L][:, :], ALU.mult).then_inc(normed[L], 1)

            def mask_kv(h, kind, base):
                pool.wait_ge(bank_drained, base + (FIL[kind]["kv", h, 1] + 1))
                pool.sem_inc(pool_gate, 1)
                for g in range(2):
                    nc.gpsimd.tensor_tensor(kvm[:, g, 0:P], kvr[:, g, 0:P], blk[:], ALU.mult).then_inc(kvm_made[h], 1)
                    nc.gpsimd.tensor_scalar(kvm[:, g, P:RD], hm[:], kvr[:, g, P:P + 1], 0.0, ALU.mult, ALU.add
                                            ).then_inc(kvm_made[h], 1)

            def scale_att(h, jj):
                for c in range(NCH):
                    pool.wait_ge(rden_made[h], jj * 2 + (c + 1))
                    tl = slice(c * (CH // P), (c + 1) * (CH // P))
                    v = kt[:, tl].rearrange("p t g (h i) -> p (t g h) i", i=DIM)
                    r = rden[:, tl].rearrange("p t g h -> p (t g h)").unsqueeze(2).to_broadcast([P, CH // P * 2 * HG, DIM])
                    nc.gpsimd.tensor_tensor(v, v, r, ALU.mult).then_inc(att_scaled[h], 1)

            def scale_w2(jf, par, f):
                if f == 0:
                    pool.wait_ge(route, jf * ROUTE + 10)
                pool.wait_ge(w2_used, jf * (NCH * FT) + (f + 1))
                pool.sem_inc(pool_gate, 1)
                nc.gpsimd.tensor_scalar(w2r[:, f % RW, :], w2s[:, f % FT, :], ews[1 - par][:, f % FT:f % FT + 1], 0.0,
                                        ALU.mult, ALU.add).then_inc(w2_scaled, 1)

            def step(kind, s, par, base):
                j = s - 2
                jf = s - 3
                for it in ORD[kind]:
                    what = it[0]
                    if what == "sums":
                        if it[1] == 0:
                            norm_sums(0, s, s, xa, xn)
                        else:
                            norm_sums(1, s, j, yrs[par], tns[par])
                    elif what == "rnorm":
                        norm_scale(it[1], (s, j)[it[1]], (LN_C_EPS, LN_T_EPS)[it[1]], kind, base)
                    elif what == "apply":
                        L = it[1]
                        norm_apply(L, (xa, yrs[par])[L], (xn, tns[par])[L], kind, base)
                    elif what == "mask":
                        mask_kv(it[1], kind, base)
                    elif what == "scale":
                        scale_att(it[1], s - 1 - it[1])
                    elif what == "proj":
                        c, m = it[1:]
                        if c == 0 and m == 0:
                            pool.wait_ge(yr_loaded, j * 16 + 16)
                        pool.wait_ge(bank_drained, base + (FIL[kind][it] + 1))
                        v = yrs[par][:, m, c * CH:(c + 1) * CH]
                        nc.gpsimd.tensor_tensor(v, v, proj_b[:, m, :], ALU.add).then_inc(y_made, 1)
                    elif what == "final":
                        c = it[1]
                        for m in range(CT):
                            pool.wait_ge(acc_drained, jf * NB + (SEED + c * CT + m + 1))
                            v = yrs[1 - par][:, m, c * CH:(c + 1) * CH]
                            nc.gpsimd.tensor_tensor(v, v, ffn_b[:, m, :], ALU.add).then_inc(out_made, 1)
                    elif what == "ffn":
                        f = it[1]
                        for g in range(0 if f == 0 else f + AHEAD, min(f + AHEAD + 1, NCH * FT)):
                            scale_w2(jf, par, g)

            run_steps(pool, step)

        @block.vector
        def _(dve):
            dve.wait_ge(w_loaded, 16 * N_W)
            nc.vector.tensor_scalar(tns[0][:, 1, 0:C], tns[0][:, 1, 0:C], BN_EPS, None, ALU.add).then_inc(setup_dve, 1)
            nc.vector.tensor_scalar(bnc[:, 3, :], bnc[:, 3, :], BN_EPS, None, ALU.add).then_inc(setup_dve, 1)
            dve.wait_ge(consts_made, 1)
            nc.vector.tensor_tensor(pw[:], pw[:], blk[:].unsqueeze(1).to_broadcast([P, QT, P]), ALU.mult
                                    ).then_inc(setup_dve, 1)
            dve.wait_ge(bn_root, 2)
            nc.vector.reciprocal(tns[0][:, 1, 0:C], tns[0][:, 1, 0:C]).then_inc(setup_dve, 1)
            nc.vector.reciprocal(bnc[:, 3, :], bnc[:, 3, :]).then_inc(setup_dve, 1)
            dve.wait_ge(setup_dve, 5)
            nc.vector.tensor_tensor(tns[0][:, 0, 0:C], tns[0][:, 0, 0:C], tns[0][:, 1, 0:C], ALU.mult).then_inc(setup_dve, 1)
            nc.vector.tensor_tensor(bnc[:, 0, :], bnc[:, 0, :], bnc[:, 3, :], ALU.mult).then_inc(setup_dve, 1)
            dve.wait_ge(setup_dve, 7)
            nc.vector.tensor_tensor(bnc[:, 2, :], bnc[:, 2, :], bnc[:, 0, :], ALU.mult).then_inc(setup_dve, 1)
            nc.vector.tensor_tensor(wp[:], wp[:], tns[0][:, 0, 0:C].unsqueeze(1).to_broadcast([P, 2 * CT, C]), ALU.mult
                                    ).then_inc(setup_dve, 1)
            dve.wait_ge(setup_dve, 8)
            nc.vector.tensor_tensor(pbias[:], bnc[:, 1, :], bnc[:, 2, :], ALU.subtract).then_inc(setup_dve, 1)
            dve.wait_ge(col_means, 1)
            af = dacc[:].rearrange("p a n -> p (a n)")
            for k in range(CT):
                nc.vector.tensor_tensor(w1s[:, k, :], w1s[:, k, :], af, ALU.subtract).then_inc(setup_dve, 1)
                nc.vector.tensor_tensor(wq[:, k, 0:CH], wq[:, k, 0:CH], wbk[0][:], ALU.subtract).then_inc(setup_dve, 1)
                nc.vector.tensor_tensor(wq[:, k, CH:QKV], wq[:, k, CH:QKV], wbk[1][:, 0:QKV - CH], ALU.subtract
                                        ).then_inc(setup_dve, 1)
                nc.vector.tensor_tensor(rws[:, k, :], rws[:, k, :], acc[:, 0, 0:NP_], ALU.subtract
                                        ).then_inc(setup_dve, 1)
            dve.wait_ge(setup_dve, 10 + 4 * CT)
            nc.vector.memset(rt[:], 0.0).then_inc(centred, 1)

            def rden_task(h, c, j, par, kind, base):
                dve.wait_ge(bank_drained, base + (FIL[kind]["att", h, (c + 1) * (CH // P) - 1] + 1))
                tl = slice(c * (CH // P), (c + 1) * (CH // P))
                nc.vector.reciprocal(rden[:, tl], den[:, tl]).then_inc(rden_made[h], 1)

            def max_task(j, kind, base):
                dve.wait_ge(bank_drained, base + (FIL[kind]["logits",] + 1))
                dve.sem_inc(dve_gate, 1)
                nc.vector.max(mx[:], lg[:]).then_inc(route, 1)
                dve.wait_ge(route, j * ROUTE + 1)
                dve.sem_inc(dve_gate, 1)
                nc.vector.max_index(ix[:], mx[:], lg[:]).then_inc(route, 1)
                nc.vector.tensor_scalar(rt[:, 0:1], mx[:, 0:1], -1.0, None, ALU.mult).then_inc(max_made, 1)

            def route_task(j):
                dve.wait_ge(exp_made, j * 2 + 2)
                nc.vector.reciprocal(rt[:, 4:5], rt[:, 1:2]).then_inc(route, 1)
                dve.wait_ge(route, j * ROUTE + 3)
                nc.vector.tensor_scalar(rt[:, 6:8], rt[:, 2:4], rt[:, 4:5], None, ALU.mult, ALU.add,
                                        accum_out=rt[:, 8:9]).then_inc(route, 1)
                nc.vector.tensor_copy(rt[:, 12:14], ix[:, 0:2]).then_inc(route, 1)
                dve.wait_ge(route, j * ROUTE + 5)
                nc.vector.reciprocal(rt[:, 9:10], rt[:, 8:9]).then_inc(route, 1)
                dve.wait_ge(route, j * ROUTE + 6)
                nc.vector.tensor_scalar(rt[:, 10:12], rt[:, 6:8], rt[:, 9:10], None, ALU.mult).then_inc(route, 1)
                dve.wait_ge(route, j * ROUTE + 7)
                for i in range(2):
                    ins = nc.vector.tensor_scalar(wsel[:, i, :], iota11[:], rt[:, 12 + i:13 + i], rt[:, 10 + i:11 + i],
                                                  ALU.is_equal, ALU.mult)
                ins.then_inc(route, 1)
                dve.wait_ge(route, j * ROUTE + 8)
                nc.vector.tensor_tensor(wsel[:, 0, :], wsel[:, 0, :], wsel[:, 1, :], ALU.add).then_inc(route, 1)
                dve.wait_ge(route, j * ROUTE + 9)

            def ew_task(j, par):
                nc.vector.tensor_tensor(ewt[:], pws[:], wsel[:, 0, :].unsqueeze(1).to_broadcast([P, FT + E, NP_]),
                                        ALU.mult).then_inc(ew_chain, 1)
                dve.wait_ge(ew_chain, j * 2 + 1)
                nc.vector.reduce_sum(ewr[:], ewt[:], axis=AX_X).then_inc(ew_chain, 1)
                dve.wait_ge(ew_chain, j * 2 + 2)
                nc.vector.scalar_tensor_tensor(out=ews[par][:], in0=ewr[:], scalar=1e-6, in1=ewr[:],
                                               op0=ALU.is_gt, op1=ALU.mult).then_inc(route, 1)
                dve.wait_ge(route, j * ROUTE + 10)
                nc.vector.tensor_tensor(obt[:], b2s[:], ews[par][:, FT:FT + E].unsqueeze(1).to_broadcast([P, CT, E]),
                                        ALU.mult).then_inc(route, 1)
                dve.wait_ge(route, j * ROUTE + 11)
                nc.vector.reduce_sum(obs[par][:], obt[:], axis=AX_X).then_inc(route, 1)
                dve.wait_ge(route, j * ROUTE + 12)
                nc.vector.tensor_copy(rt[:, 14:15], rt[:, 8:9]).then_inc(route, 1)

            TASKS = {30: (2, lambda *a: rden_task(1, 0, *a)), 33: (2, lambda *a: rden_task(1, 1, *a)),
                     66: (1, lambda *a: rden_task(0, 0, *a)), 69: (1, lambda *a: rden_task(0, 1, *a)),
                     98: (2, lambda j, p, k, b: max_task(j, k, b)),
                     104: (2, lambda j, p, k, b: (route_task(j), ew_task(j, p)))}

            def step(kind, s, par, base):
                j = s - 2
                if not kind[1]:
                    for t in sorted(TASKS):
                        stage, task = TASKS[t]
                        if kind[stage]:
                            task(j, par, kind, base)
                    return
                d = (s - 1) * DW_OPS
                n = 0
                for pair in range(QT // 2):
                    for i, tap in enumerate(TAP_ORDER + [None]):
                        if tap is not None:
                            dy, dx = tap // TAPS - TAPS // 2, tap % TAPS - TAPS // 2
                        oy, iy, ny = max(0, -dy), max(0, dy), HH - abs(dy)
                        ox, ixx, nx = max(0, -dx), max(0, dx), WW - abs(dx)
                        for m in (2 * pair, 2 * pair + 1):
                            if n in TASKS and kind[TASKS[n][0]]:
                                TASKS[n][1](j, par, kind, base)
                            a3 = dacc[:, m % 2, :].rearrange("p (y x) -> p y x", x=WW)
                            o3 = dwo[:, m, :].rearrange("p (y x) -> p y x", x=WW)
                            i3 = qkvs[:, m, :].rearrange("p (y x) -> p y x", x=WW)
                            w = dww[:, m, tap:tap + 1] if tap is not None else None
                            if n > 0 or past(s, 2):
                                if n > 1 or past(s, 2):
                                    dve.wait_ge(taps, d + (n - 1))
                            if i == 0:
                                if m % 2 == 0:
                                    if pair < 2:
                                        dve.wait_ge(bank_drained, base - tail(("qkv", 2 * pair + 1, NCH - 1)))
                                    else:
                                        dve.wait_ge(bank_drained, base + (FIL[kind]["qkv", 5, NCH - 1] + 1))
                                ins = nc.vector.tensor_scalar(dacc[:, m % 2, :], qkvs[:, m, :], w, None, ALU.mult)
                            elif tap is None:
                                ins = nc.vector.tensor_copy(o3[:, :, WW - 1:WW], a3[:, :, WW - 1:WW])
                            else:
                                dst = a3
                                if tap == LAST_TAP:
                                    dst = o3
                                    if kind[2] and m % 2 == 0:
                                        dve.wait_ge(bank_filled, base + (FIL[kind]["agg", 2 * pair + 1, NCH - 1] + 1))
                                ins = nc.vector.scalar_tensor_tensor(
                                    out=dst[:, oy:oy + ny, ox:ox + nx], in0=i3[:, iy:iy + ny, ixx:ixx + nx], scalar=w,
                                    in1=a3[:, oy:oy + ny, ox:ox + nx], op0=ALU.mult, op1=ALU.add)
                            ins.then_inc(taps, 1)
                            n += 1

            run_steps(dve, step)


def partition_table():
    partitions = [(6,), (5, 1), (4, 2), (4, 1, 1), (3, 3), (3, 2, 1), (3, 1, 1, 1), (2, 2, 2), (2, 2, 1, 1),
                  (2, 1, 1, 1, 1), (1, 1, 1, 1, 1, 1)]
    w = np.zeros((NP_, E), np.float32)
    for i, part in enumerate(partitions):
        for k, size in enumerate(part):
            w[i, k] = size / 6
    table = np.zeros((P, FT + E, NP_), np.float32)
    for t in range(FT):
        for p in range(P):
            f = t * P + p
            if f < E * F:
                table[p, t] = w[:, f // F]
    table[:, FT:] = w.T[None]
    return table.reshape(P, (FT + E) * NP_)


def kernel(x, L0_conv_qkv_w, L0_conv_agg_dw_w, L0_conv_agg_pw_w, L0_conv_proj_w, L0_conv_bn_gamma, L0_conv_bn_beta,
           L0_conv_bn_mean, L0_conv_bn_var, L0_ffn_router_w, L0_ffn_W1, L0_ffn_b1, L0_ffn_W2, L0_ffn_b2):
    import concourse.bacc as bacc
    from concourse.bass_utils import run_bass_kernel_spmd

    def by_part(a):
        a = np.asarray(a)
        return a.reshape(C // DIM, 3, DIM, -1).transpose(1, 0, 2, 3).reshape(QKV, -1)

    w1 = np.zeros((C, FT * P), np.float32)
    w1[:, :E * F] = np.asarray(L0_ffn_W1).transpose(1, 0, 2).reshape(C, E * F)
    b1 = np.zeros((FT * P,), np.float32)
    b1[:E * F] = np.asarray(L0_ffn_b1).reshape(-1)
    w2 = np.zeros((FT * P, C), np.float32)
    w2[:E * F] = np.asarray(L0_ffn_W2).reshape(E * F, C)
    gamma, beta, mean, var = (np.asarray(a) for a in (L0_conv_bn_gamma, L0_conv_bn_beta, L0_conv_bn_mean,
                                                      L0_conv_bn_var))
    arrays = {
        "x": np.asarray(x).reshape(B, C, T),
        "w_qkv": by_part(L0_conv_qkv_w).T,
        "w_dw": by_part(L0_conv_agg_dw_w),
        "w_pw": by_part(L0_conv_agg_pw_w).T,
        "w_proj": np.asarray(L0_conv_proj_w).reshape(C, 2 * C).T,
        "bn": np.stack([gamma, beta, mean, var]).reshape(4, CT, P).transpose(2, 0, 1),
        "bn_rows": np.stack([gamma, var]),
        "w_router": np.asarray(L0_ffn_router_w).T,
        "w1": w1,
        "b1": b1.reshape(FT, P).T,
        "w2": w2,
        "b2": np.asarray(L0_ffn_b2).T,
        "parts": partition_table(),
    }
    arrays = {n: np.ascontiguousarray(a) for n, a in arrays.items()}
    nc = bacc.Bacc("TRN2", target_bir_lowering=False, num_devices=1, dynamic_dma_scratch_size=1024)
    args = [nc.dram_tensor(n, a.shape, F32, kind="ExternalInput").ap() for n, a in arrays.items()]
    out = nc.dram_tensor("out", (B, C, T), F32, kind="ExternalOutput").ap()
    build(nc, *args, out)
    r = run_bass_kernel_spmd(nc, [arrays], core_ids=[0])
    return np.asarray(r.results[0]["out"]).reshape(B, C, HH, WW)
```

```python
import numpy as np

from contextlib import ExitStack

import concourse.bass as bass
from concourse import mybir

F32 = mybir.dt.float32
F16 = mybir.dt.float16
U32 = mybir.dt.uint32
ALU = mybir.AluOpType
ACT = mybir.ActivationFunctionType
AX_X = mybir.AxisListType.X

P = 128
B, C, HH, WW = 8, 256, 32, 32
T = HH * WW
CT = C // P
QKV = 3 * C
QT = QKV // P
DIM = 8
TAPS = 5
E, F = 6, 341
FT = (E * F + P - 1) // P
NP_ = 11
CH = 512
NCH = T // CH
TT = T // P
HG = P // DIM
RD = P + HG
WB = 2
GB = 4
LAG = 3
X_SCALE, W_SCALE, G_SCALE = 256.0, 64.0, 16.0
LN_C_EPS, LN_T_EPS, ATT_EPS, BN_EPS = 1e-6, 1e-5, 1e-15, 1e-5

CENTER = (TAPS // 2) * TAPS + TAPS // 2
LAST_TAP = CENTER + 1
BASE_TAPS = [CENTER + TAPS, CENTER - TAPS, CENTER - 1, CENTER + 2 * TAPS, CENTER - 2 * TAPS, CENTER - 2]


def base_taps(first, m):
    return (0 if m < 2 else len(BASE_TAPS)) if first else 3


def tap_order(first, pair):
    skip = BASE_TAPS[:base_taps(first, 2 * pair)] + [CENTER, LAST_TAP]
    return [CENTER] + [t for t in range(TAPS * TAPS) if t not in skip] + [LAST_TAP, None]


def tap_ops(first, pair):
    return sum(2 * len(tap_order(first, p)) for p in range(pair))


def schedule(a, d, c, f):
    o = []
    todo = list(range(NCH * FT)) if f else []

    def second(n):
        o.append(("second", n))
        if n % FT == FT - 1:
            o.append(("final", n // FT))

    def ffn(k):
        for _ in range(k):
            if todo:
                n = todo.pop(0)
                o.append(("ffn", n))
                if n > 0:
                    o.append(("gsplit", n - 1))
                if n >= LAG:
                    second(n - LAG)

    def with_base(items):
        for item in items:
            o.append(item)
            o.extend(waiting[:at_a_time])
            del waiting[:at_a_time]

    def qkv(m):
        with_base(("qkv", m, ch) for ch in range(NCH))

    def agg(*ms):
        o.extend(("agg", m, ch) for m in ms for ch in range(NCH))

    first = d and not c
    waiting = [("base", 1, m, i) for m in range(2, QT) for i in range(base_taps(first, m))] if d else []
    at_a_time = 6 if first else 1

    def spread_out(items, every):
        for n, item in enumerate(items):
            o.append(item)
            if n % every == every - 1:
                ffn(1)

    if d:
        qkv(4)
        qkv(5)
    ffn(1)
    if a:
        o.extend([("squares", 0), ("sums", 0)])
    if a and not d:
        o.append(("weights", 0))
    if c:
        agg(4, 5)
        at_a_time = 2
        with_base([("kv", 1, 0), ("kv", 1, 1)])
        at_a_time = 1
        o.append(("mask", 1))
    if a:
        o.append(("stats", 0, 0))
    ffn(1)
    if a:
        o.extend([("stats", 0, 1), ("rnorm", 0)])
    if c:
        spread_out([("att", 1, t) for t in range(TT)], 1)
        o.append(("scale", 1))
    ffn(1)
    if a:
        o.extend([("rbc", 0, ch) for ch in range(NCH)] + [("apply", 0)])
    if a and not d:
        o.append(("weights", 1))
    ffn(1)
    if c:
        o.extend(("back", 1, ch, g) for ch in range(NCH) for g in range(2))
    if a:
        o.extend([("high", 0), ("low", 0)])
    if c:
        with_base(("proj", ch, m) for ch in range(NCH) for m in range(CT))
    if d:
        o.append(("relu_q",))
        spread_out([("tok", t) for t in range(2)], 1)
    if c:
        o.extend([("squares", 1), ("sums", 1)])
    if d:
        spread_out([("tok", t) for t in range(2, TT)], 1)
        with_base([("kv", 0, 0), ("kv", 0, 1)])
        o.append(("mask", 0))
    if c:
        o.extend([("stats", 1, 0), ("rnorm", 1)])
    ffn(1)
    if d:
        spread_out([("att", 0, t) for t in range(TT)], 1)
        o.append(("scale", 0))
    if c:
        o.extend([("rbc", 1, ch) for ch in range(NCH)] + [("apply", 1)])
    ffn(2)
    if d:
        o.extend(("back", 0, ch, g) for ch in range(NCH) for g in range(2))
    if c:
        o.extend([("high", 1), ("low", 1)])
    ffn(1)
    if c:
        o.append(("usum",))
    if a:
        qkv(0)
        qkv(1)
    if c:
        o.append(("logits",))
    ffn(1)
    o.extend(waiting)
    if d:
        agg(0, 1)
    waiting = [("base", 0, m, i) for m in range(2) for i in range(base_taps(not d, m))] if a else []
    ffn(2)
    if a:
        qkv(2)
    if d:
        with_base(("agg", m, ch) for m in (2, 3) for ch in range(NCH))
    o.extend(waiting)
    if c and not a:
        o.append(("exp",))
    ffn(len(todo))
    if f:
        o.append(("gsplit", NCH * FT - 1))
        second(NCH * FT - LAG)
    for ch in range(NCH):
        if a:
            o.append(("qkv", 3, ch))
        if f:
            second(NCH * FT - LAG + 1 + ch)
    if c and a:
        o.append(("exp",))
    return o


BANKED = ("qkv", "agg", "kv", "stats", "rbc", "att", "back", "proj", "tok", "logits", "ffn")


def fills(order):
    return {it: n for n, it in enumerate([it for it in order if it[0] in BANKED])}


def past(s, k):
    return not isinstance(s, int) or s >= k


def build(nc, x, w_qkv, w_dw, w_pw, w_proj, bn, bn_rows, w_router, w1, b1, w2, b2, parts, out):
    with ExitStack() as ctx:
        def sb(name, shape, dt=F32):
            return ctx.enter_context(nc.sbuf_tensor(name, shape, dt))

        def sem(name):
            return ctx.enter_context(nc.semaphore(name))

        wqh, wql = (sb(n, [P, CT, QKV], F16) for n in ("wqh", "wql"))
        w1h, w1l = (sb(n, [P, CT, FT * P], F16) for n in ("w1h", "w1l"))
        w2h, w2l = (sb(n, [P, FT, C], F16) for n in ("w2h", "w2l"))
        wp = sb("wp", [P, 2 * CT, C])
        pw = sb("pw", [P, QT, P])
        dww = sb("dww", [P, QT, TAPS * TAPS])
        b1s = sb("b1s", [P, FT])
        b2s = sb("b2s", [P, CT, E])
        rws = sb("rws", [P, CT, NP_])
        pws = sb("pws", [P, FT + E, NP_])
        bnc = sb("bnc", [P, 4, CT])
        ident = sb("ident", [P, P])
        blk = sb("blk", [P, P])
        hm = sb("hm", [P, HG])
        mean_w = sb("mean_w", [P, P])
        spread = sb("spread", [P, P])
        iota11 = sb("iota11", [P, NP_])
        pbias = sb("pbias", [P, CT])
        xa = sb("xa", [P, CT, T])
        nrm = sb("nrm", [P, CT, T])
        xh, xl = (sb(n, [P, CT, T], F16) for n in ("xh", "xl"))
        yrs = [sb(f"yr{i}", [P, CT, T]) for i in range(2)]
        ths, tls = ([sb(f"{n}{i}", [P, CT, T], F16) for i in range(2)] for n in ("th", "tl"))
        rb = sb("rb", [P, T])
        qkvs = sb("qkvs", [P, QT, T])
        dwo = sb("dwo", [P, QT, T])
        qr = sb("qr", [P, 2, T])
        kt = sb("kt", [P, TT, 2, P])
        vt = sb("vt", [P, TT, 2, P + 2])
        ac = sb("ac", [P, 2, T])
        kvr = sb("kvr", [P, 2, P + 1])
        kvm = sb("kvm", [P, 2, RD])
        tapb = sb("tapb", [P, 2, T])
        den = sb("den", [P, TT, 2, HG])
        sum_b = sb("sum_b", [P, 2, CH])
        hb = sb("hb", [P, GB, CH])
        gh, gl = (sb(n, [P, GB, CH], F16) for n in ("gh", "gl"))
        st = [sb(f"st{i}", [P, 2, TT]) for i in range(2)]
        sv = [sb(f"sv{i}", [P, 4, TT]) for i in range(2)]
        mhalf = sb("mhalf", [P, TT])
        us = sb("us", [P, CT])
        lg = sb("lg", [P, 16])
        mx = sb("mx", [P, 8])
        ix = sb("ix", [P, 8], U32)
        rt = sb("rt", [P, 16])
        ex = sb("ex", [P, 16])
        wsel = sb("wsel", [P, 2, NP_])
        ewt = sb("ewt", [P, FT + E, NP_])
        ewr = sb("ewr", [P, FT + E])
        ews = [sb(f"ew{i}", [P, FT + E]) for i in range(2)]
        obt = sb("obt", [P, CT, E])
        ewg = [sb(f"ewg{i}", [P, FT + E]) for i in range(2)]
        obs = [sb(f"ob{i}", [P, CT]) for i in range(2)]

        w1r = dwo[:, 0:4, :].rearrange("p (k a) n -> p k (a n)", k=CT)
        wqr = dwo[:, 4:6, :].rearrange("p a n -> p (a n)")[:, 0:CT * QKV].rearrange("p (k n) -> p k n", k=CT)
        w2r = [yr[:].rearrange("p a (t n) -> p (a t) n", n=C) for yr in yrs]
        bnr = qr[:, :, 0:C]

        dacc = ctx.enter_context(nc.psum_tensor("dacc", [P, 2, T], F32))
        acc = ctx.enter_context(nc.psum_tensor("acc", [P, CT, CH], F32))
        wbk = [ctx.enter_context(nc.psum_tensor(f"wbk{i}", [P, CH], F32)) for i in range(WB)]

        wq_loaded = sem("wq_loaded")
        w1_loaded = sem("w1_loaded")
        bn_loaded = sem("bn_loaded")
        w_loaded = sem("w_loaded")
        x_loaded = sem("x_loaded")
        yr_loaded = sem("yr_loaded")
        w2_loaded = sem("w2_loaded")
        out_stored = sem("out_stored")
        mean_made = sem("mean_made")
        consts_made = sem("consts_made")
        setup_pool = sem("setup_pool")
        q_means = sem("q_means")
        w1_means = sem("w1_means")
        q_centred = sem("q_centred")
        w1_centred = sem("w1_centred")
        q_high = sem("q_high")
        w_high = sem("w_high")
        q_split = sem("q_split")
        weights_ready = sem("weights_ready")
        bn_root = sem("bn_root")
        setup_dve = sem("setup_dve")
        bank_filled = sem("bank_filled")
        bank_drained = sem("bank_drained")
        squared = [sem(f"squared{i}") for i in range(2)]
        summed = [sem(f"summed{i}") for i in range(2)]
        ln_chain = [sem(f"ln_chain{i}") for i in range(2)]
        diag_made = [sem(f"diag_made{i}") for i in range(2)]
        normed = [sem(f"normed{i}") for i in range(2)]
        high_made = [sem(f"high_made{i}") for i in range(2)]
        low_made = [sem(f"low_made{i}") for i in range(2)]
        taps = sem("taps")
        tap_scaled = sem("tap_scaled")
        tap_added = sem("tap_added")
        kvm_made = [sem(f"kvm_made{i}") for i in range(2)]
        rden_made = [sem(f"rden_made{i}") for i in range(2)]
        att_scaled = [sem(f"att_scaled{i}") for i in range(2)]
        q_relued = sem("q_relued")
        y_made = sem("y_made")
        u_made = sem("u_made")
        max_made = sem("max_made")
        exp_made = sem("exp_made")
        route = sem("route")
        g_high = sem("g_high")
        g_scaled = sem("g_scaled")
        g_low = sem("g_low")
        summed_up = sem("summed_up")
        acc_drained = sem("acc_drained")
        out_made = sem("out_made")
        ew_chain = sem("ew_chain")
        pool_gate = sem("pool_gate")
        dve_gate = sem("dve_gate")
        SEED = 4
        NB = CT * NCH
        ROUTE = 13

        block = ctx.enter_context(nc.Block())

        KINDS = [(1, 0, 0, 0), (1, 1, 0, 0), (1, 1, 1, 0), (1, 1, 1, 1), (0, 1, 1, 1), (0, 0, 1, 1), (0, 0, 0, 1)]
        FULL = KINDS[3]
        ORD = {k: schedule(*k) for k in KINDS}
        FIL = {k: fills(o) for k, o in ORD.items()}
        NF = {k: len(f) for k, f in FIL.items()}
        assert all(n % WB == 0 for n in NF.values()) and B % 2 == 0

        def tail(kind, s, it):
            before = FULL if kind == FULL and past(s, 4) else KINDS[KINDS.index(kind) - 1]
            return NF[before] - (FIL[before][it] + 1)

        def is_first(j):
            return isinstance(j, int) and j == 0

        def taps_done(j, pair):
            if is_first(j):
                return tap_ops(True, pair)
            return j * tap_ops(False, QT // 2) + (tap_ops(True, QT // 2) - tap_ops(False, QT // 2)
                                                  + tap_ops(False, pair))

        def base_done(j, m):
            def before(first, m):
                return sum(base_taps(first, i) for i in range(m))
            if is_first(j):
                return before(True, m)
            return j * before(False, QT) + (before(True, QT) - before(False, QT) + before(False, m))

        def drained_qkv(kind, s, base, d, m):
            if d == 1 and m < 4:
                return base - tail(kind, s, ("qkv", m, NCH - 1))
            return base + (FIL[kind]["qkv", m, NCH - 1] + 1)

        def clip(tap):
            dy, dx = tap // TAPS - TAPS // 2, tap % TAPS - TAPS // 2
            oy, iy, ny = max(0, -dy), max(0, dy), HH - abs(dy)
            ox, ix, nx = max(0, -dx), max(0, dx), WW - abs(dx)
            return (slice(oy, oy + ny), slice(ox, ox + nx)), (slice(iy, iy + ny), slice(ix, ix + nx))

        def run_steps(eng, step, peeled=4):
            base = 0
            for s in range(peeled):
                step(KINDS[min(s, 3)], s, s % 2, base)
                base += NF[KINDS[min(s, 3)]]
            pairs = (B - 4) // 2
            with eng.Fori(0, pairs) as it:
                step(FULL, it * 2 + peeled, peeled % 2, it * (2 * NF[FULL]) + base)
                step(FULL, it * 2 + (peeled + 1), 1 - peeled % 2, it * (2 * NF[FULL]) + (base + NF[FULL]))
            base += 2 * pairs * NF[FULL]
            for s in range(peeled + 2 * pairs, B + 3):
                kind = KINDS[max(3, 4 + s - B)]
                step(kind, s, s % 2, base)
                base += NF[kind]

        @block.sync
        def _(sp):
            sp.dma_start(wqr, w_qkv.rearrange("(k p) n -> p k n", p=P)).then_inc(wq_loaded, 16)
            sp.dma_start(xa[:], x[0].rearrange("(k p) n -> p k n", p=P)).then_inc(x_loaded, 16)
            sp.dma_start(w1r, w1.rearrange("(k p) n -> p k n", p=P)).then_inc(w1_loaded, 16)
            sp.dma_start(rws[:], w_router.rearrange("(k p) n -> p k n", p=P)).then_inc(w1_loaded, 16)
            sp.dma_start(bnc[:], bn).then_inc(bn_loaded, 16)
            for i in range(2):
                sp.dma_start(bnr[:, i, :], bn_rows[i:i + 1, :].to_broadcast([P, C])).then_inc(bn_loaded, 16)
            sp.dma_start(wp[:], w_proj.rearrange("(k p) n -> p k n", p=P)).then_inc(bn_loaded, 16)
            for i in range(2):
                sp.dma_start(w2r[i], w2.rearrange("(i t p) n -> i p t n", p=P, i=2)[i]).then_inc(w2_loaded, 16)
            sp.dma_start(dww[:], w_dw.rearrange("(k p) n -> p k n", p=P)).then_inc(w_loaded, 16)
            for g in range(HG):
                sp.dma_start(pw[g * DIM:(g + 1) * DIM, :, :], w_pw.rearrange("i (m n) -> i m n", m=QT)
                             ).then_inc(w_loaded, 16)
            sp.dma_start(b2s[:], b2.rearrange("(k p) n -> p k n", p=P)).then_inc(w_loaded, 16)
            sp.dma_start(b1s[:], b1).then_inc(w_loaded, 16)
            sp.dma_start(pws[:], parts.rearrange("p (t n) -> p t n", n=NP_)).then_inc(w_loaded, 16)
            sp.wait_ge(weights_ready, 1)
            for i in range(2):
                sp.dma_start(yrs[i][:], x[i].rearrange("(k p) n -> p k n", p=P)).then_inc(yr_loaded, 16)

            def step(kind, s, par, base):
                if kind[0] and (not isinstance(s, int) or s < B - 1):
                    sp.wait_ge(normed[0], s * 2 + 2)
                    sp.dma_start(xa[:], x[bass.ds(s + 1, 1)].rearrange("o (k p) n -> p (o k) n", p=P)
                                 ).then_inc(x_loaded, 16)
                if kind[3]:
                    jf = s - 3
                    yr = yrs[1 - par]
                    for c in range(NCH):
                        sp.wait_ge(out_made, jf * NB + (SEED + (c + 1) * CT))
                        sp.dma_start(out[bass.ds(jf, 1), :, c * CH:(c + 1) * CH].rearrange("o (k p) n -> p (o k) n", p=P),
                                     yr[:, :, c * CH:(c + 1) * CH]).then_inc(out_stored, 16)
                    if not isinstance(s, int) or s <= B:
                        sp.wait_ge(out_stored, jf * (16 * NCH) + 16 * NCH)
                        sp.dma_start(yr[:], x[bass.ds(s - 1, 1)].rearrange("o (k p) n -> p (o k) n", p=P)
                                     ).then_inc(yr_loaded, 16)

            run_steps(sp, step, peeled=3)
            sp.wait_ge(out_stored, B * NCH * 16)

        @block.tensor
        def _(pe):
            pe.wait_ge(wq_loaded, 16)
            pe.wait_ge(mean_made, 1)
            for dst, lo, hi in ((wbk[0][:, :], 0, CH), (wbk[1][:, 0:QKV - CH], CH, QKV)):
                for k in range(CT):
                    last = nc.tensor.matmul(dst, mean_w[:], wqr[:, k, lo:hi], start=(k == 0), stop=(k == CT - 1))
            last.then_inc(q_means, 1)
            pe.wait_ge(w1_loaded, 32)
            af = dacc[:].rearrange("p a (b n) -> p (a b) n", n=CH)
            for n in range(FT * P // CH):
                for k in range(CT):
                    nc.tensor.matmul(af[:, n, :], mean_w[:], w1r[:, k, n * CH:(n + 1) * CH],
                                     start=(k == 0), stop=(k == CT - 1))
            for k in range(CT):
                last = nc.tensor.matmul(acc[:, 0, 0:NP_], mean_w[:], rws[:, k, :], start=(k == 0), stop=(k == CT - 1))
            last.then_inc(w1_means, 1)
            pe.wait_ge(q_centred, 4)
            pe.wait_ge(consts_made, 1)

            def step(kind, s, par, base):
                j = s - 2
                jf = s - 3
                n = 0
                if kind == KINDS[1]:
                    pe.wait_ge(weights_ready, 1)
                for it in ORD[kind]:
                    what = it[0]
                    if what == "second":
                        second(kind, jf, base, it[1])
                        continue
                    if what not in BANKED:
                        continue
                    if not isinstance(base, int) or base + n - (WB - 1) > 0:
                        pe.wait_ge(bank_drained, base + (n - (WB - 1)))
                    b = wbk[n % WB]
                    n += 1
                    if what == "qkv":
                        m, c = it[1:]
                        if m == 0 and c == 0:
                            pe.wait_ge(low_made[0], s * 2 + 2)
                            if kind == KINDS[0]:
                                pe.wait_ge(q_split, 1)
                        last = split_product(b[:], wqh, wql, xh, xl, m, c)
                    elif what == "agg":
                        m, c = it[1:]
                        if m % 2 == 0 and c == 0:
                            jj = j if m == 4 else s - 1
                            pe.wait_ge(taps, taps_done(jj, m // 2 + 1))
                        if m < 2:
                            last = nc.tensor.matmul(b[:], pw[:, m, :], dwo[:, m, c * CH:(c + 1) * CH],
                                                    start=True, stop=True)
                        else:
                            for i in range(CH // P):
                                o = c * CH + i * P
                                last = nc.tensor.matmul(b[:, i * P:(i + 1) * P], dwo[:, m, o:o + P], pw[:, m, :],
                                                        start=True, stop=True)
                    elif what == "tok":
                        t = it[1]
                        if t == 0:
                            pe.wait_ge(bank_drained, base + (FIL[kind]["qkv", 5, NCH - 1] + 1))
                        for i in range(4):
                            last = nc.tensor.transpose(b[:, i * P:(i + 1) * P], qkvs[:, 2 + i, t * P:(t + 1) * P],
                                                       ident[:])
                    elif what == "kv":
                        h, g = it[1:]
                        if g == 0:
                            src = ("agg", 5, NCH - 1) if h else ("tok", TT - 1)
                            pe.wait_ge(bank_drained, base + (FIL[kind][src] + 1))
                        for t in range(TT):
                            last = nc.tensor.matmul(b[:, 0:P + 1], kt[:, t, g, :], vt[:, t, g, 0:P + 1],
                                                    start=(t == 0), stop=(t == TT - 1))
                    elif what == "att":
                        h, t = it[1:]
                        if t == 0:
                            pe.wait_ge(kvm_made[h], (s - 1 - h) * 4 + 4)
                            if h == 0:
                                pe.wait_ge(q_relued, s * 2)
                        for g in range(2):
                            last = nc.tensor.matmul(b[:, g * RD:(g + 1) * RD], qr[:, g, t * P:(t + 1) * P],
                                                    kvm[:, g, :], start=True, stop=True)
                    elif what == "back":
                        h, c, g = it[1:]
                        if g == 0:
                            pe.wait_ge(att_scaled[h], (s - 1 - h) * 2 + (c + 1))
                        for i in range(CH // P):
                            last = nc.tensor.transpose(b[:, i * P:(i + 1) * P], kt[:, c * (CH // P) + i, g, :],
                                                       ident[:])
                    elif what == "proj":
                        c, m = it[1:]
                        if c == 0 and m == 0:
                            pe.wait_ge(bank_drained, base + (FIL[kind]["back", 1, NCH - 1, 1] + 1))
                        for k in range(2 * CT):
                            last = nc.tensor.matmul(b[:], wp[:, k, m * P:(m + 1) * P],
                                                    (ac, qr)[k // CT][:, k % CT, c * CH:(c + 1) * CH],
                                                    start=(k == 0), stop=(k == 2 * CT - 1))
                    elif what == "stats":
                        L, i = it[1:]
                        jj = s if L == 0 else j
                        src = (0,) if (L == 0 and i == 0) else (1,) if L == 0 else (0, 1)
                        for q in src:
                            pe.wait_ge(summed[L], jj * 2 + (q + 1))
                            data = rb[:, :] if q == 0 else nrm[:, 0, :]
                            for t in range(TT):
                                last = nc.tensor.matmul(b[:, q * TT + t:q * TT + t + 1], data[:, t * P:(t + 1) * P],
                                                        mean_w[:, 0:1], start=True, stop=True)
                    elif what == "rbc":
                        L, c = it[1:]
                        if c == 0:
                            pe.wait_ge(diag_made[L], (s if L == 0 else j) + 1)
                        last = nc.tensor.matmul(b[:], spread[:], rb[:, c * CH:(c + 1) * CH], start=True, stop=True)
                    elif what == "logits":
                        pe.wait_ge(u_made, j * 2 + 2)
                        for k in range(CT):
                            last = nc.tensor.matmul(b[:, 0:NP_], us[:, k:k + 1].to_broadcast([P, P]), rws[:, k, :],
                                                    start=(k == 0), stop=(k == CT - 1))
                    elif what == "ffn":
                        f = it[1]
                        c, t = f // FT, f % FT
                        if f == 0:
                            pe.wait_ge(low_made[1], jf * 2 + 2)
                        last = split_product(b[:], w1h, w1l, ths[1 - par], tls[1 - par], t, c)
                    last.then_inc(bank_filled, 1)

            def split_product(dst, wh, wl, dh, dl, m, c):
                parts = [(w, d, k) for w, d in ((wh, dh), (wh, dl), (wl, dh)) for k in range(CT)]
                for i, (w, d, k) in enumerate(parts):
                    last = nc.tensor.matmul(dst, w[:, k, m * P:(m + 1) * P], d[:, k, c * CH:(c + 1) * CH],
                                            start=(i == 0), stop=(i == len(parts) - 1))
                return last

            def second(kind, jf, base, f):
                c, t = f // FT, f % FT
                pe.wait_ge(g_low, jf * (NCH * FT) + (f + 1))
                if t == 0:
                    pe.wait_ge(acc_drained, jf * NB + (SEED + c * CT))
                for m in range(CT):
                    for i, (w, d) in enumerate(((w2h, gh), (w2h, gl), (w2l, gh))):
                        last = nc.tensor.matmul(acc[:, m, :], w[:, t, m * P:(m + 1) * P], d[:, f % GB, :],
                                                start=(t == 0 and i == 0), stop=(t == FT - 1 and i == 2),
                                                skip_group_check=True)
                if t == FT - 1:
                    last.then_inc(summed_up, 1)

            run_steps(pe, step)

        @block.scalar
        def _(act):
            act.wait_ge(consts_made, 1)
            act.sem_inc(acc_drained, SEED)

            def step(kind, s, par, base):
                j = s - 2
                jf = s - 3
                yr = yrs[par]
                n = 0
                if kind == KINDS[1]:
                    act.wait_ge(weights_ready, 1)
                for it in ORD[kind]:
                    what = it[0]
                    if what == "weights":
                        if it[1] == 0:
                            act.wait_ge(q_centred, 4)
                            nc.scalar.activation(wqh[:], wqr, ACT.Copy, scale=W_SCALE).then_inc(q_high, 1)
                            act.wait_ge(setup_dve, 2)
                            nc.scalar.activation(bnr[:, 1, :], bnr[:, 1, :], ACT.Sqrt).then_inc(bn_root, 1)
                            nc.scalar.activation(bnc[:, 3, :], bnc[:, 3, :], ACT.Sqrt).then_inc(bn_root, 1)
                        else:
                            act.wait_ge(w1_centred, 4)
                            nc.scalar.activation(w1h[:], w1r, ACT.Copy, scale=W_SCALE).then_inc(w_high, 1)
                            act.wait_ge(w2_loaded, 32)
                            for i in range(2):
                                nc.scalar.activation(w2h[:, i * (FT // 2):(i + 1) * (FT // 2)], w2r[i], ACT.Copy,
                                                     scale=W_SCALE).then_inc(w_high, 1)
                        continue
                    if what == "base":
                        d, m, i = it[1:]
                        jj = s - d
                        done = base_done(jj, m)
                        x3 = qkvs[:, m, :].rearrange("p (y x) -> p y x", x=WW)
                        w = dww[:, m, BASE_TAPS[i]:BASE_TAPS[i] + 1]
                        if i == 0:
                            act.wait_ge(bank_drained, drained_qkv(kind, s, base, d, m))
                            (oy, ox), (iy, ix) = clip(BASE_TAPS[0])
                            d3 = dwo[:, m, :].rearrange("p (y x) -> p y x", x=WW)
                            ins = nc.scalar.activation(d3[:, oy, :], x3[:, iy, :], ACT.Copy, scale=w)
                        else:
                            if not (is_first(jj) and done == 0 and i == 1):
                                act.wait_ge(tap_added, done + (i - 1))
                            ins = nc.scalar.activation(tapb[:, i % 2, :], qkvs[:, m, :], ACT.Copy, scale=w)
                        ins.then_inc(tap_scaled, 1)
                        continue
                    if what == "high":
                        L = it[1]
                        for m in range(CT):
                            act.wait_ge(normed[L], (j if L else s) * 2 + (m + 1))
                            nc.scalar.activation((ths[par] if L else xh)[:, m, :], nrm[:, m, :], ACT.Copy
                                                 ).then_inc(high_made[L], 1)
                        continue
                    if what == "gsplit":
                        f = it[1]
                        if f == 0:
                            act.wait_ge(route, jf * ROUTE + ROUTE)
                        act.wait_ge(bank_drained, base + (FIL[kind]["ffn", f] + 1))
                        w = ewg[1 - par][:, f % FT:f % FT + 1]
                        nc.scalar.activation(gh[:, f % GB, :], hb[:, f % GB, :], ACT.Copy, scale=w).then_inc(g_high, 1)
                        continue
                    if what == "squares":
                        L = it[1]
                        if L == 0:
                            act.wait_ge(x_loaded, s * 16 + 16)
                        for m in range(CT):
                            if L == 1:
                                act.wait_ge(y_made, j * NB + NB)
                            elif past(s, 3):
                                act.wait_ge(low_made[1], s * 2 - 4)
                            nc.scalar.activation(nrm[:, m, :], (xa, yr)[L][:, m, :], ACT.Square).then_inc(squared[L], 1)
                        continue
                    if what == "relu_q":
                        for g in range(2):
                            nc.scalar.activation(qr[:, g, :], qkvs[:, g, :], ACT.Relu).then_inc(q_relued, 1)
                        continue
                    if what == "usum":
                        for m in range(CT):
                            act.wait_ge(normed[1], j * 2 + 2)
                            if m:
                                act.wait_ge(u_made, j * 2 + m)
                            nc.scalar.activation(rb[:, :], nrm[:, m, :], ACT.Copy, scale=1.0 / (T * X_SCALE),
                                                 accum_out=us[:, m:m + 1]).then_inc(u_made, 1)
                        continue
                    if what == "exp":
                        act.wait_ge(max_made, j + 1)
                        nc.scalar.activation(ex[:, 0:NP_], lg[:, 0:NP_], ACT.Exp, bias=rt[:, 0:1],
                                             accum_out=rt[:, 1:2]).then_inc(exp_made, 1)
                        nc.scalar.activation(rt[:, 2:4], mx[:, 0:2], ACT.Exp, bias=rt[:, 0:1]).then_inc(exp_made, 1)
                        continue
                    if what == "final":
                        c = it[1]
                        act.wait_ge(summed_up, jf * NCH + (c + 1))
                        for m in range(CT):
                            if c == 0 and kind[2]:
                                act.wait_ge(y_made, j * NB + NB)
                            act.wait_ge(out_made, jf * NB + (SEED + c * CT + m - 1))
                            nc.scalar.activation(sum_b[:, m, :], acc[:, m, :], ACT.Identity,
                                                 scale=1.0 / (W_SCALE * G_SCALE),
                                                 bias=obs[1 - par][:, m:m + 1]).then_inc(acc_drained, 1)
                        continue
                    if what not in BANKED:
                        continue
                    act.wait_ge(bank_filled, base + (n + 1))
                    b = wbk[n % WB]
                    n += 1
                    if what == "qkv":
                        m, c = it[1:]
                        if c == 0 and m % 2 == 0:
                            if m == 4 and past(s, 2):
                                act.wait_ge(taps, taps_done(j, 3))
                            if m < 4 and past(s, 1):
                                act.wait_ge(taps, taps_done(s - 1, m // 2 + 1))
                            if m == 0 and past(s, 1):
                                act.wait_ge(q_relued, s * 2)
                        last = nc.scalar.activation(qkvs[:, m, c * CH:(c + 1) * CH], b[:], ACT.Copy,
                                                    scale=1.0 / (X_SCALE * W_SCALE))
                    elif what == "agg":
                        m, c = it[1:]
                        tl = slice(c * (CH // P), (c + 1) * (CH // P))
                        bt = b[:].rearrange("p (t n) -> p t n", n=P)
                        if m < 2:
                            last = nc.scalar.activation(qr[:, m, c * CH:(c + 1) * CH], b[:], ACT.Relu)
                        elif m < 4:
                            last = nc.scalar.activation(kt[:, tl, m - 2, :], bt, ACT.Relu)
                        else:
                            last = nc.scalar.activation(vt[:, tl, m - 4, 0:P], bt, ACT.Copy)
                    elif what == "tok":
                        t = it[1]
                        bt = b[:].rearrange("p (a g n) -> p a g n", a=2, g=2)
                        nc.scalar.activation(kt[:, t, :, :], bt[:, 0], ACT.Relu)
                        last = nc.scalar.activation(vt[:, t, :, 0:P], bt[:, 1], ACT.Copy)
                    elif what == "kv":
                        last = nc.scalar.activation(kvr[:, it[2], :], b[:, 0:P + 1], ACT.Copy)
                    elif what == "att":
                        t = it[2]
                        bt = b[:, 0:2 * RD].rearrange("p (g n) -> p g n", g=2)
                        nc.scalar.activation(kt[:, t, :, :], bt[:, :, 0:P], ACT.Copy)
                        last = nc.scalar.activation(den[:, t, :, :], bt[:, :, P:RD], ACT.Copy, bias=ATT_EPS)
                    elif what == "back":
                        h, c, g = it[1:]
                        last = nc.scalar.activation((ac, qr)[h][:, g, c * CH:(c + 1) * CH], b[:], ACT.Copy)
                    elif what == "proj":
                        c, m = it[1:]
                        if c > 0:
                            act.wait_ge(y_made, j * NB + (c * CT + m - 1))
                        elif kind[3]:
                            act.wait_ge(out_made, jf * NB + SEED)
                        last = nc.scalar.activation(sum_b[:, m, :], b[:], ACT.Identity, bias=pbias[:, m:m + 1])
                    elif what == "stats":
                        L, i = it[1:]
                        if L == 0:
                            last = nc.scalar.activation(st[0][:, i, :], b[:, i * TT:(i + 1) * TT], ACT.Copy)
                        else:
                            last = nc.scalar.activation(st[1][:].rearrange("p a b -> p (a b)"), b[:, 0:2 * TT], ACT.Copy)
                    elif what == "rbc":
                        L, c = it[1:]
                        last = nc.scalar.activation(rb[:, c * CH:(c + 1) * CH], b[:], ACT.Copy)
                    elif what == "logits":
                        last = nc.scalar.activation(lg[:, 0:NP_], b[:, 0:NP_], ACT.Copy)
                    elif what == "ffn":
                        f = it[1]
                        last = nc.scalar.activation(hb[:, f % GB, :], b[:], ACT.Gelu, bias=b1s[:, f % FT:f % FT + 1],
                                                    scale=1.0 / (X_SCALE * W_SCALE))
                    last.then_inc(bank_drained, 1)

            run_steps(act, step)

        @block.gpsimd
        def _(pool):
            chain = [0]

            def after(ins):
                chain[0] += 1
                ins.then_inc(setup_pool, 1)
                pool.wait_ge(setup_pool, chain[0])

            nc.gpsimd.memset(mean_w[:], 1.0 / C).then_inc(mean_made, 1)
            after(nc.gpsimd.memset(ident[:], 0.0))
            after(nc.gpsimd.affine_select(out=ident[:], in_=ident[:], compare_op=ALU.not_equal, fill=1.0, base=0,
                                          pattern=[[-1, P]], channel_multiplier=1))
            for tile, w in ((blk[:].rearrange("p (h i) -> p h i", i=DIM), DIM), (hm[:].unsqueeze(2), 1)):
                after(nc.gpsimd.memset(tile, 1.0))
                after(nc.gpsimd.affine_select(out=tile, in_=tile, compare_op=ALU.is_ge, fill=0.0, base=0,
                                              pattern=[[-DIM, HG], [0, w]], channel_multiplier=1))
                after(nc.gpsimd.affine_select(out=tile, in_=tile, compare_op=ALU.is_ge, fill=0.0, base=DIM - 1,
                                              pattern=[[DIM, HG], [0, w]], channel_multiplier=-1))
            after(nc.gpsimd.memset(spread[:], X_SCALE))
            after(nc.gpsimd.memset(mhalf[:], -0.5))
            after(nc.gpsimd.memset(lg[:], -3.0e38))
            after(nc.gpsimd.memset(vt[:, :, :, P:P + 2], 1.0))
            after(nc.gpsimd.iota(iota11[:], pattern=[[1, NP_]], base=0, channel_multiplier=0,
                                 allow_small_or_imprecise_dtypes=True))
            nc.gpsimd.memset(ex[:], 0.0).then_inc(consts_made, 1)
            pool.sem_inc(out_made, SEED)

            def norm_sums(L, s, jj, src):
                if L == 0:
                    pool.wait_ge(x_loaded, jj * 16 + 16)
                else:
                    pool.wait_ge(y_made, jj * NB + NB)
                if past(s, 3):
                    pool.wait_ge(u_made, s * 2 - 4)
                nc.gpsimd.tensor_tensor(rb[:, :], src[:, 0, :], src[:, 1, :], ALU.add).then_inc(summed[L], 1)
                pool.wait_ge(squared[L], jj * 2 + 2)
                nc.gpsimd.tensor_tensor(nrm[:, 0, :], nrm[:, 0, :], nrm[:, 1, :], ALU.add).then_inc(summed[L], 1)

            def norm_scale(L, jj, eps, kind, base):
                pool.wait_ge(bank_drained, base + (FIL[kind]["stats", L, 1 - L] + 1))
                m, q = st[L][:, 0, :], st[L][:, 1, :]
                nc.gpsimd.tensor_tensor(sv[L][:, 0, :], m, m, ALU.mult).then_inc(ln_chain[L], 1)
                pool.wait_ge(ln_chain[L], jj * 4 + 1)
                nc.gpsimd.tensor_tensor(sv[L][:, 1, :], q, sv[L][:, 0, :], ALU.subtract).then_inc(ln_chain[L], 1)
                pool.wait_ge(ln_chain[L], jj * 4 + 2)
                pool.sem_inc(pool_gate, 1)
                nc.gpsimd.tensor_scalar(sv[L][:, 2, :], sv[L][:, 1, :], 1.0, eps, ALU.mult, ALU.add
                                        ).then_inc(ln_chain[L], 1)
                pool.wait_ge(ln_chain[L], jj * 4 + 3)
                nc.gpsimd.tensor_tensor(sv[L][:, 3, :], sv[L][:, 2, :], mhalf[:], ALU.pow).then_inc(ln_chain[L], 1)
                pool.wait_ge(ln_chain[L], jj * 4 + 4)
                nc.gpsimd.tensor_tensor(rb[:].rearrange("p (t n) -> p t n", n=P),
                                        ident[:].unsqueeze(1).to_broadcast([P, TT, P]),
                                        sv[L][:, 3, :].unsqueeze(2).to_broadcast([P, TT, P]),
                                        ALU.mult).then_inc(diag_made[L], 1)

            def norm_apply(L, src, kind, base):
                pool.wait_ge(bank_drained, base + (FIL[kind]["rbc", L, NCH - 1] + 1))
                for m in range(CT):
                    nc.gpsimd.tensor_tensor(nrm[:, m, :], src[:, m, :], rb[:, :], ALU.mult).then_inc(normed[L], 1)

            def mask_kv(h, kind, base):
                pool.wait_ge(bank_drained, base + (FIL[kind]["kv", h, 1] + 1))
                pool.sem_inc(pool_gate, 1)
                for g in range(2):
                    nc.gpsimd.tensor_tensor(kvm[:, g, 0:P], kvr[:, g, 0:P], blk[:], ALU.mult).then_inc(kvm_made[h], 1)
                    nc.gpsimd.tensor_scalar(kvm[:, g, P:RD], hm[:], kvr[:, g, P:P + 1], 0.0, ALU.mult, ALU.add
                                            ).then_inc(kvm_made[h], 1)

            def scale_att(h, jj):
                for c in range(NCH):
                    pool.wait_ge(rden_made[h], jj * 2 + (c + 1))
                    tl = slice(c * (CH // P), (c + 1) * (CH // P))
                    v = kt[:, tl].rearrange("p t g (h i) -> p (t g h) i", i=DIM)
                    r = den[:, tl].rearrange("p t g h -> p (t g h)").unsqueeze(2).to_broadcast([P, CH // P * 2 * HG, DIM])
                    nc.gpsimd.tensor_tensor(v, v, r, ALU.mult).then_inc(att_scaled[h], 1)

            def lows(L, jj, high, low):
                for m in range(CT):
                    pool.wait_ge(high_made[L], jj * 2 + (m + 1))
                    nc.gpsimd.tensor_tensor(low[:, m, :], nrm[:, m, :], high[:, m, :], ALU.subtract
                                            ).then_inc(low_made[L], 1)

            def step(kind, s, par, base):
                j = s - 2
                jf = s - 3
                for it in ORD[kind]:
                    what = it[0]
                    if what == "sums":
                        norm_sums(it[1], s, (s, j)[it[1]], (xa, yrs[par])[it[1]])
                    elif what == "base":
                        d, m, i = it[1:]
                        done = base_done(s - d, m)
                        pool.wait_ge(tap_scaled, done + (i + 1))
                        d3 = dwo[:, m, :].rearrange("p (y x) -> p y x", x=WW)
                        if i == 0:
                            pool.sem_inc(pool_gate, 1)
                            ins = nc.gpsimd.memset(d3[:, HH - 1:HH, :], 0.0)
                        else:
                            pool.wait_ge(tap_added, done + i)
                            (oy, ox), (iy, ix) = clip(BASE_TAPS[i])
                            t3 = tapb[:, i % 2, :].rearrange("p (y x) -> p y x", x=WW)
                            ins = nc.gpsimd.tensor_tensor(d3[:, oy, ox], d3[:, oy, ox], t3[:, iy, ix], ALU.add)
                        ins.then_inc(tap_added, 1)
                    elif what == "low":
                        L = it[1]
                        lows(L, (s, j)[L], (xh, ths[par])[L], (xl, tls[par])[L])
                    elif what == "rnorm":
                        norm_scale(it[1], (s, j)[it[1]], (LN_C_EPS, LN_T_EPS)[it[1]], kind, base)
                    elif what == "apply":
                        L = it[1]
                        norm_apply(L, (xa, yrs[par])[L], kind, base)
                    elif what == "mask":
                        mask_kv(it[1], kind, base)
                    elif what == "scale":
                        scale_att(it[1], s - 1 - it[1])
                    elif what == "proj":
                        c, m = it[1:]
                        if c == 0 and m == 0:
                            pool.wait_ge(yr_loaded, j * 16 + 16)
                        pool.wait_ge(bank_drained, base + (FIL[kind][it] + 1))
                        v = yrs[par][:, m, c * CH:(c + 1) * CH]
                        nc.gpsimd.tensor_tensor(v, v, sum_b[:, m, :], ALU.add).then_inc(y_made, 1)
                    elif what == "final":
                        c = it[1]
                        for m in range(CT):
                            pool.wait_ge(acc_drained, jf * NB + (SEED + c * CT + m + 1))
                            v = yrs[1 - par][:, m, c * CH:(c + 1) * CH]
                            nc.gpsimd.tensor_tensor(v, v, sum_b[:, m, :], ALU.add).then_inc(out_made, 1)
                    elif what == "gsplit":
                        f = it[1]
                        pool.wait_ge(g_high, jf * (NCH * FT) + (f + 1))
                        pool.sem_inc(pool_gate, 1)
                        nc.gpsimd.tensor_scalar(hb[:, f % GB, :], hb[:, f % GB, :], ewg[1 - par][:, f % FT:f % FT + 1],
                                                0.0, ALU.mult, ALU.add).then_inc(g_scaled, 1)
                        pool.wait_ge(g_scaled, jf * (NCH * FT) + (f + 1))
                        nc.gpsimd.tensor_tensor(gl[:, f % GB, :], hb[:, f % GB, :], gh[:, f % GB, :], ALU.subtract
                                                ).then_inc(g_low, 1)

            run_steps(pool, step)

        @block.vector
        def _(dve):
            dve.wait_ge(q_means, 1)
            for k in range(CT):
                nc.vector.tensor_tensor(wqr[:, k, 0:CH], wqr[:, k, 0:CH], wbk[0][:], ALU.subtract).then_inc(q_centred, 1)
                nc.vector.tensor_tensor(wqr[:, k, CH:QKV], wqr[:, k, CH:QKV], wbk[1][:, 0:QKV - CH], ALU.subtract
                                        ).then_inc(q_centred, 1)
            dve.wait_ge(bn_loaded, 64)
            nc.vector.tensor_scalar(bnr[:, 1, :], bnr[:, 1, :], BN_EPS, None, ALU.add).then_inc(setup_dve, 1)
            nc.vector.tensor_scalar(bnc[:, 3, :], bnc[:, 3, :], BN_EPS, None, ALU.add).then_inc(setup_dve, 1)
            dve.wait_ge(q_high, 1)
            nc.vector.scalar_tensor_tensor(out=wql[:], in0=wqr, scalar=W_SCALE, in1=wqh[:],
                                           op0=ALU.mult, op1=ALU.subtract).then_inc(q_split, 1)
            dve.wait_ge(w1_means, 1)
            for k in range(CT):
                nc.vector.tensor_tensor(w1r[:, k, :], w1r[:, k, :], dacc[:].rearrange("p a n -> p (a n)"), ALU.subtract
                                        ).then_inc(w1_centred, 1)
                nc.vector.tensor_tensor(rws[:, k, :], rws[:, k, :], acc[:, 0, 0:NP_], ALU.subtract
                                        ).then_inc(w1_centred, 1)
            dve.wait_ge(bn_root, 2)
            nc.vector.reciprocal(bnr[:, 1, :], bnr[:, 1, :]).then_inc(setup_dve, 1)
            nc.vector.reciprocal(bnc[:, 3, :], bnc[:, 3, :]).then_inc(setup_dve, 1)
            dve.wait_ge(setup_dve, 4)
            nc.vector.tensor_tensor(bnr[:, 0, :], bnr[:, 0, :], bnr[:, 1, :], ALU.mult).then_inc(setup_dve, 1)
            nc.vector.tensor_tensor(bnc[:, 0, :], bnc[:, 0, :], bnc[:, 3, :], ALU.mult).then_inc(setup_dve, 1)
            dve.wait_ge(setup_dve, 6)
            nc.vector.tensor_tensor(bnc[:, 2, :], bnc[:, 2, :], bnc[:, 0, :], ALU.mult).then_inc(setup_dve, 1)
            nc.vector.tensor_tensor(wp[:], wp[:], bnr[:, 0, :].unsqueeze(1).to_broadcast([P, 2 * CT, C]), ALU.mult
                                    ).then_inc(setup_dve, 1)
            dve.wait_ge(setup_dve, 7)
            nc.vector.tensor_tensor(pbias[:], bnc[:, 1, :], bnc[:, 2, :], ALU.subtract).then_inc(setup_dve, 1)
            dve.wait_ge(w_high, 1)
            nc.vector.scalar_tensor_tensor(out=w1l[:], in0=w1r, scalar=W_SCALE, in1=w1h[:],
                                           op0=ALU.mult, op1=ALU.subtract).then_inc(setup_dve, 1)
            dve.wait_ge(w_high, 3)
            for i in range(2):
                tl = slice(i * (FT // 2), (i + 1) * (FT // 2))
                nc.vector.scalar_tensor_tensor(out=w2l[:, tl], in0=w2r[i], scalar=W_SCALE, in1=w2h[:, tl],
                                               op0=ALU.mult, op1=ALU.subtract).then_inc(setup_dve, 1)
            dve.wait_ge(consts_made, 1)
            dve.wait_ge(w_loaded, 16 * (4 + HG))
            nc.vector.tensor_tensor(pw[:], pw[:], blk[:].unsqueeze(1).to_broadcast([P, QT, P]), ALU.mult
                                    ).then_inc(setup_dve, 1)
            dve.wait_ge(setup_dve, 13)
            nc.vector.memset(rt[:], 0.0).then_inc(weights_ready, 1)

            def rden_task(h, c, j, par, kind, base):
                dve.wait_ge(bank_drained, base + (FIL[kind]["att", h, (c + 1) * (CH // P) - 1] + 1))
                tl = slice(c * (CH // P), (c + 1) * (CH // P))
                nc.vector.reciprocal(den[:, tl], den[:, tl]).then_inc(rden_made[h], 1)

            def max_task(j, drained):
                dve.wait_ge(bank_drained, drained)
                dve.sem_inc(dve_gate, 1)
                nc.vector.max(mx[:], lg[:]).then_inc(route, 1)
                dve.wait_ge(route, j * ROUTE + 1)
                dve.sem_inc(dve_gate, 1)
                nc.vector.max_index(ix[:], mx[:], lg[:]).then_inc(route, 1)
                nc.vector.tensor_scalar(rt[:, 0:1], mx[:, 0:1], -1.0, None, ALU.mult).then_inc(max_made, 1)

            def route_task(j):
                dve.wait_ge(exp_made, j * 2 + 2)
                nc.vector.reciprocal(rt[:, 4:5], rt[:, 1:2]).then_inc(route, 1)
                dve.wait_ge(route, j * ROUTE + 3)
                nc.vector.tensor_scalar(rt[:, 6:8], rt[:, 2:4], rt[:, 4:5], None, ALU.mult, ALU.add,
                                        accum_out=rt[:, 8:9]).then_inc(route, 1)
                nc.vector.tensor_copy(rt[:, 12:14], ix[:, 0:2]).then_inc(route, 1)
                dve.wait_ge(route, j * ROUTE + 5)
                nc.vector.reciprocal(rt[:, 9:10], rt[:, 8:9]).then_inc(route, 1)
                dve.wait_ge(route, j * ROUTE + 6)
                nc.vector.tensor_scalar(rt[:, 10:12], rt[:, 6:8], rt[:, 9:10], None, ALU.mult).then_inc(route, 1)
                dve.wait_ge(route, j * ROUTE + 7)
                for i in range(2):
                    ins = nc.vector.tensor_scalar(wsel[:, i, :], iota11[:], rt[:, 12 + i:13 + i], rt[:, 10 + i:11 + i],
                                                  ALU.is_equal, ALU.mult)
                ins.then_inc(route, 1)
                dve.wait_ge(route, j * ROUTE + 8)
                nc.vector.tensor_tensor(wsel[:, 0, :], wsel[:, 0, :], wsel[:, 1, :], ALU.add).then_inc(route, 1)
                dve.wait_ge(route, j * ROUTE + 9)

            def ew_task(j, par):
                nc.vector.tensor_tensor(ewt[:], pws[:], wsel[:, 0, :].unsqueeze(1).to_broadcast([P, FT + E, NP_]),
                                        ALU.mult).then_inc(ew_chain, 1)
                dve.wait_ge(ew_chain, j * 2 + 1)
                nc.vector.reduce_sum(ewr[:], ewt[:], axis=AX_X).then_inc(ew_chain, 1)
                dve.wait_ge(ew_chain, j * 2 + 2)
                nc.vector.scalar_tensor_tensor(out=ews[par][:], in0=ewr[:], scalar=1e-6, in1=ewr[:],
                                               op0=ALU.is_gt, op1=ALU.mult).then_inc(route, 1)
                dve.wait_ge(route, j * ROUTE + 10)
                nc.vector.tensor_tensor(obt[:], b2s[:], ews[par][:, FT:FT + E].unsqueeze(1).to_broadcast([P, CT, E]),
                                        ALU.mult).then_inc(route, 1)
                dve.wait_ge(route, j * ROUTE + 11)
                nc.vector.reduce_sum(obs[par][:], obt[:], axis=AX_X).then_inc(route, 1)
                dve.wait_ge(route, j * ROUTE + 12)
                nc.vector.tensor_scalar(ewg[par][:], ews[par][:], G_SCALE, None, ALU.mult).then_inc(route, 1)

            def route_tasks(j, par):
                route_task(j)
                ew_task(j, par)

            DIVIDE = {44: (2, 1, 0), 47: (2, 1, 1), 104: (1, 0, 0), 107: (1, 0, 1)}
            CARRIED = {8: "max", 16: "route"}
            OWN = {128: "max", 136: "route"}

            def small_tasks(n, kind, s, par, base):
                j = s - 2
                if n in DIVIDE and kind[DIVIDE[n][0]]:
                    rden_task(DIVIDE[n][1], DIVIDE[n][2], j, par, kind, base)
                if n in CARRIED and kind[3]:
                    if CARRIED[n] == "max":
                        max_task(j - 1, base - tail(kind, s, ("logits",)))
                    else:
                        route_tasks(j - 1, 1 - par)
                if n in OWN and kind[2] and not kind[0]:
                    if OWN[n] == "max":
                        max_task(j, base + (FIL[kind]["logits",] + 1))
                    else:
                        route_tasks(j, par)

            def step(kind, s, par, base):
                j = s - 2
                if not kind[1]:
                    for n in sorted(list(DIVIDE) + list(OWN)):
                        small_tasks(n, kind, s, par, base)
                    return
                jj = s - 1
                first = is_first(jj)
                d = taps_done(jj, 0)
                n = 0
                for pair in range(QT // 2):
                    for tap in tap_order(first, pair):
                        for m in (2 * pair, 2 * pair + 1):
                            small_tasks(n, kind, s, par, base)
                            a3 = dacc[:, m % 2, :].rearrange("p (y x) -> p y x", x=WW)
                            o3 = dwo[:, m, :].rearrange("p (y x) -> p y x", x=WW)
                            i3 = qkvs[:, m, :].rearrange("p (y x) -> p y x", x=WW)
                            if not first or n > 1:
                                dve.wait_ge(taps, d + (n - 1))
                            if tap is None:
                                ins = nc.vector.tensor_copy(o3[:, :, WW - 1:WW], a3[:, :, WW - 1:WW])
                            elif tap == CENTER:
                                w = dww[:, m, tap:tap + 1]
                                if base_taps(first, m):
                                    dve.wait_ge(tap_added, base_done(jj, m + 1))
                                    ins = nc.vector.scalar_tensor_tensor(out=dacc[:, m % 2, :], in0=qkvs[:, m, :],
                                                                         scalar=w, in1=dwo[:, m, :],
                                                                         op0=ALU.mult, op1=ALU.add)
                                else:
                                    dve.wait_ge(bank_drained, drained_qkv(kind, s, base, 1, m))
                                    ins = nc.vector.tensor_scalar(dacc[:, m % 2, :], qkvs[:, m, :], w, None, ALU.mult)
                            else:
                                (oy, ox), (iy, ix) = clip(tap)
                                dst = o3 if tap == LAST_TAP else a3
                                ins = nc.vector.scalar_tensor_tensor(
                                    out=dst[:, oy, ox], in0=i3[:, iy, ix], scalar=dww[:, m, tap:tap + 1],
                                    in1=a3[:, oy, ox], op0=ALU.mult, op1=ALU.add)
                            ins.then_inc(taps, 1)
                            n += 1

            run_steps(dve, step)


def partition_table():
    partitions = [(6,), (5, 1), (4, 2), (4, 1, 1), (3, 3), (3, 2, 1), (3, 1, 1, 1), (2, 2, 2), (2, 2, 1, 1),
                  (2, 1, 1, 1, 1), (1, 1, 1, 1, 1, 1)]
    w = np.zeros((NP_, E), np.float32)
    for i, part in enumerate(partitions):
        for k, size in enumerate(part):
            w[i, k] = size / 6
    table = np.zeros((P, FT + E, NP_), np.float32)
    for t in range(FT):
        for p in range(P):
            f = t * P + p
            if f < E * F:
                table[p, t] = w[:, f // F]
    table[:, FT:] = w.T[None]
    return table.reshape(P, (FT + E) * NP_)


def kernel(x, L0_conv_qkv_w, L0_conv_agg_dw_w, L0_conv_agg_pw_w, L0_conv_proj_w, L0_conv_bn_gamma, L0_conv_bn_beta,
           L0_conv_bn_mean, L0_conv_bn_var, L0_ffn_router_w, L0_ffn_W1, L0_ffn_b1, L0_ffn_W2, L0_ffn_b2):
    import concourse.bacc as bacc
    from concourse.bass_utils import run_bass_kernel_spmd

    def by_part(a):
        a = np.asarray(a)
        return a.reshape(C // DIM, 3, DIM, -1).transpose(1, 0, 2, 3).reshape(QKV, -1)

    w1 = np.zeros((C, FT * P), np.float32)
    w1[:, :E * F] = np.asarray(L0_ffn_W1).transpose(1, 0, 2).reshape(C, E * F)
    b1 = np.zeros((FT * P,), np.float32)
    b1[:E * F] = np.asarray(L0_ffn_b1).reshape(-1)
    w2 = np.zeros((FT * P, C), np.float32)
    w2[:E * F] = np.asarray(L0_ffn_W2).reshape(E * F, C)
    gamma, beta, mean, var = (np.asarray(a) for a in (L0_conv_bn_gamma, L0_conv_bn_beta, L0_conv_bn_mean,
                                                      L0_conv_bn_var))
    arrays = {
        "x": np.asarray(x).reshape(B, C, T),
        "w_qkv": by_part(L0_conv_qkv_w).T,
        "w_dw": by_part(L0_conv_agg_dw_w),
        "w_pw": by_part(L0_conv_agg_pw_w).T,
        "w_proj": np.asarray(L0_conv_proj_w).reshape(C, 2 * C).T,
        "bn": np.stack([gamma, beta, mean, var]).reshape(4, CT, P).transpose(2, 0, 1),
        "bn_rows": np.stack([gamma, var]),
        "w_router": np.asarray(L0_ffn_router_w).T,
        "w1": w1,
        "b1": b1.reshape(FT, P).T,
        "w2": w2,
        "b2": np.asarray(L0_ffn_b2).T,
        "parts": partition_table(),
    }
    arrays = {n: np.ascontiguousarray(a) for n, a in arrays.items()}
    nc = bacc.Bacc("TRN2", target_bir_lowering=False, num_devices=1, dynamic_dma_scratch_size=1024)
    args = [nc.dram_tensor(n, a.shape, F32, kind="ExternalInput").ap() for n, a in arrays.items()]
    out = nc.dram_tensor("out", (B, C, T), F32, kind="ExternalOutput").ap()
    build(nc, *args, out)
    r = run_bass_kernel_spmd(nc, [arrays], core_ids=[0])
    return np.asarray(r.results[0]["out"]).reshape(B, C, HH, WW)
```
